# Optimizing a Trainium2 kernel written in Bass

```python
import numpy as np
import jax
import jax.numpy as jnp

def _softmax(x, axis=-1):
    return jax.nn.softmax(x, axis=axis)

def _gelu(x):
    return jax.nn.gelu(x, approximate=True)

def _silu(x):
    return jax.nn.silu(x)

def _sigmoid(x):
    return jax.nn.sigmoid(x)

def _layernorm(x, axis=-1, eps=1e-05):
    m = jnp.mean(x, axis=axis, keepdims=True)
    v = jnp.var(x, axis=axis, keepdims=True)
    return (x - m) / jnp.sqrt(v + eps)

def _scatter_add(tgt, idx, src, axis=0):
    return tgt.at[idx].add(src)

def _segment_sum(src, seg, n):
    return jax.ops.segment_sum(src, seg, n)
kernel_name = 'mk_adaln_ffn_d1_seqx_r4_71960d'

def setup_inputs(seed: int=0):
    np.random.seed(seed)
    _w = jnp.asarray

    def _rec_inputs():
        import jax
        import jax.numpy as jnp
        _rk = jax.random.key(seed)
        x = -0.000125 + 0.9999 * jax.random.normal(jax.random.fold_in(_rk, 1), (64, 64, 1024), jnp.float32)
        _lenS = 64 - jax.random.randint(jax.random.fold_in(_rk, 7), (64,), 0, max(1, 64 // 4) + 1, jnp.int32)
        _lenS2 = 64 - jax.random.randint(jax.random.fold_in(_rk, 8), (64,), 0, max(1, 64 // 4) + 1, jnp.int32)
        cond_128 = 0.0061147 + 1.02565 * jax.random.normal(jax.random.fold_in(_rk, 11), (64, 128), jnp.float32)
        fside_S_0 = -0.022604 + 0.987366 * jax.random.normal(jax.random.fold_in(_rk, 12), (64,), jnp.float32)
        return (x, cond_128, fside_S_0)
    x, cond_128, fside_S_0 = _rec_inputs()

    def _L0_cond_setup():
        import jax, jax.numpy as jnp
        import numpy as np
        from jax import lax
        N, C_IN, L = (32, 64, 1024)
        C_OUT, K, GROUPS = (64, 9, 4)
        C_DIM, PAD, STRIDE = (128, 4, 1)
        key = jax.random.key(seed)
        k1, k2, k3, k4, k5 = jax.random.split(key, 5)
        x = jax.random.normal(k1, (N, C_IN, L), dtype=jnp.float32)
        c = jax.random.normal(k2, (N, C_DIM), dtype=jnp.float32)
        weight = jax.random.normal(k3, (C_OUT, C_IN // GROUPS, K), dtype=jnp.float32)
        c_weight = jax.random.normal(k4, (C_OUT, C_DIM), dtype=jnp.float32)
        bias = jax.random.normal(k5, (C_OUT,), dtype=jnp.float32)
        return {'x': x, 'c': c, 'weight': weight, 'c_weight': c_weight, 'bias': bias}
    _L0_cond_all = _L0_cond_setup()
    _L0_cond_in = {k: v for k, v in _L0_cond_all.items() if k in ('weight', 'c_weight')}
    del _L0_cond_all

    def _L0_ffn_setup():
        import jax, jax.numpy as jnp
        import numpy as np
        C_CLAMP = 0.5
        EPS = 1e-06
        key = jax.random.key(seed)
        ks = jax.random.split(key, 6)
        B_, S, D, O, R, E = (4, 512, 1024, 1024, 16, 8)
        x = jax.random.normal(ks[0], (B_, S, D), dtype=jnp.float32)
        W = jax.random.normal(ks[1], (O, D), dtype=jnp.float32) * (1.0 / np.sqrt(D))
        b = jax.random.normal(ks[2], (O,), dtype=jnp.float32) * 0.01
        A = jax.random.normal(ks[3], (E, D, R), dtype=jnp.float32) * (1.0 / np.sqrt(D))
        Bm = jax.random.normal(ks[4], (E, R, O), dtype=jnp.float32) * (1.0 / np.sqrt(R))
        p_scores = jax.random.uniform(ks[5], (E,), dtype=jnp.float32)
        return {'x': x, 'W': W, 'b': b, 'A': A, 'B': Bm, 'p_scores': p_scores}
    _L0_ffn_all = _L0_ffn_setup()
    _L0_ffn_in = {k: v for k, v in _L0_ffn_all.items() if k in ('W', 'b', 'A', 'B', 'p_scores')}
    del _L0_ffn_all
    return {'x': x, 'cond_128': cond_128, 'fside_S_0': fside_S_0, 'L0_cond_weight': _L0_cond_in['weight'], 'L0_cond_c_weight': _L0_cond_in['c_weight'], 'L0_ffn_W': _L0_ffn_in['W'], 'L0_ffn_b': _L0_ffn_in['b'], 'L0_ffn_A': _L0_ffn_in['A'], 'L0_ffn_B': _L0_ffn_in['B'], 'L0_ffn_p_scores': _L0_ffn_in['p_scores']}

def reference(x, cond_128, fside_S_0, L0_cond_weight, L0_cond_c_weight, L0_ffn_W, L0_ffn_b, L0_ffn_A, L0_ffn_B, L0_ffn_p_scores):
    import jax
    import jax.numpy as jnp

    def _L0_cond_ref(x, c, weight, c_weight, bias):
        import jax, jax.numpy as jnp
        import numpy as np
        from jax import lax
        N, C_IN, L = (32, 64, 1024)
        C_OUT, K, GROUPS = (64, 9, 4)
        C_DIM, PAD, STRIDE = (128, 4, 1)
        out = lax.conv_general_dilated(x, weight, window_strides=(STRIDE,), padding=[(PAD, PAD)], dimension_numbers=('NCH', 'OIH', 'NCH'), feature_group_count=GROUPS)
        ctx = jnp.einsum('nd,od->no', c, c_weight)
        out = out + ctx[:, :, None] + bias[None, :, None]
        return out

    def _L0_ffn_ref(x, W, b, A, B, p_scores):
        import jax, jax.numpy as jnp
        import numpy as np
        C_CLAMP = 0.5
        EPS = 1e-06
        z = jnp.einsum('bsd,od->bso', x, W) + b
        u = jnp.einsum('bsd,edr->ebsr', x, A)
        m = jnp.einsum('ebsr,ero,e->bso', u, B, p_scores)
        norm_z = jnp.linalg.norm(z, axis=-1, keepdims=True)
        norm_m = jnp.linalg.norm(m, axis=-1, keepdims=True)
        gamma = jnp.minimum(C_CLAMP * norm_z / (norm_m + EPS), 1.0)
        return z + gamma * m
    x = x + _L0_ffn_ref(_L0_cond_ref(x, cond_128, L0_cond_weight, L0_cond_c_weight, fside_S_0), L0_ffn_W, L0_ffn_b, L0_ffn_A, L0_ffn_B, L0_ffn_p_scores)
    return x

_drawn_inputs = setup_inputs


def setup_inputs(seed=0):
    import zlib

    import numpy as np

    out = dict(_drawn_inputs(seed))
    spreads = {}
    factors = {'L0_ffn_b': 64.0}
    for name, (base, spread) in spreads.items():
        noise = np.random.default_rng([zlib.crc32(name.encode()), seed]).standard_normal(out[name].shape)
        drawn = base * np.exp(spread * noise) if base else spread * noise
        out[name] = jnp.asarray(drawn.astype(out[name].dtype))
    for name, factor in factors.items():
        out[name] = (out[name] * factor).astype(out[name].dtype)
    return out
```

```python
from contextlib import ExitStack

import concourse.bass as bass
from concourse import mybir

F32 = mybir.dt.float32
F32R = mybir.dt.float32r
BF16 = mybir.dt.bfloat16
ALU = mybir.AluOpType
ACT = mybir.ActivationFunctionType
AX_X = mybir.AxisListType.X

P = 128
BANK = 512
C_CLAMP = 0.5
EPS = 1e-6


def build(nc, x, cond, bias, conv_w, cond_w, ffn_w, ffn_b, ffn_a, ffn_bm, p_scores, out):
    N, C, L = x.shape
    CO, CI, K = conv_w.shape
    G = C // CI
    OG = CO // G
    PAD = K // 2
    S = P // CI
    J = L // S
    D = cond.shape[1]
    O = ffn_w.shape[0]
    E, _, R = ffn_a.shape
    ER = E * R
    NB = 4
    W2 = NB * C // P
    NT = NB // W2
    STEPS = N // NB
    XP = L + 2 * PAD
    JE = J + 2
    OB = O // P
    H = O // BANK
    SLOTS = 2 * S + S - 1
    assert J == P and OG * S == P and ER == P and S == 2 * PAD and H == 2 and G == NB == 4

    x_tiles = x.rearrange("(t w n) c l -> (t w) (n c) l", w=W2, n=NT)
    out_tiles = out.rearrange("(t w n) c l -> (t w) (n c) l", w=W2, n=NT)

    with ExitStack() as ctx:
        def sb(name, shape, dt=F32):
            return ctx.enter_context(nc.sbuf_tensor(name, shape, dt))

        def sem(name):
            return ctx.enter_context(nc.semaphore(name))

        wt_hi, wt_lo = (sb(f"wt_{h}", [P, S, O], F32R) for h in ("hi", "lo"))
        a_hi, a_lo = (sb(f"a_{h}", [P, S, ER], F32R) for h in ("hi", "lo"))
        pb_hi, pb_lo = (sb(f"pb_{h}", [P, O], F32R) for h in ("hi", "lo"))
        toep_hi, toep_lo = (sb(f"toep_{h}", [P, G, 2, P], F32R) for h in ("hi", "lo"))
        row_add = sb("row_add", [P, G, N])
        b_rows = sb("b_rows", [P, O])
        x_in = sb("x_in", [P, W2, XP])
        x_keep = sb("x_keep", [P, 2, W2, L])
        xT = sb("xT", [P, NB * G, S, CI])
        xs_hi, xs_lo = (sb(f"xs_{h}", [P, G, NB, JE], F32R) for h in ("hi", "lo"))
        y = sb("y", [P, G, NB, J])
        yT_hi, yT_lo = (sb(f"yT_{h}", [P, 2, S, W2 * P], F32R) for h in ("hi", "lo"))
        u_hi, u_lo = (sb(f"u_{h}", [P, W2 * P], F32R) for h in ("hi", "lo"))
        zb = sb("zb", [P, W2, O])
        squares = sb("squares", [P, O], BF16)
        ident = sb("ident", [P, P])
        same_i = sb("same_i", [P, CI])
        same_ng = sb("same_ng", [P, P // CI])
        edge_l = sb("edge_l", [P, W2, S, CI])
        half = sb("half", [P, 2])
        ssq = sb("ssq", [P, W2, 2])
        norms = sb("norms", [P, W2, 2])
        den = sb("den", [P, W2])
        rden = sb("rden", [P, W2])
        gamma = sb("gamma", [P, W2])
        shifts = zb[0:CI, :, :].rearrange("p w c -> p (w c)")[:, 0:SLOTS * CO].rearrange(
            "p (m o) -> p m o", o=CO)
        conv_nat = sb("conv_nat", [CO, CI * K])
        cond_nat = sb("cond_nat", [N, D])
        cond_w_nat = sb("cond_w_nat", [CO, D])
        condT = sb("condT", [D, N + CO])
        cw_wide = y[:, 2, :, :].rearrange("p (g a) j -> p g (a j)", g=G).rearrange("p g (q o) -> p g q o", q=S)
        bias_wide = y[0:1, 3, :, :].rearrange("p (g a) j -> p g (a j)", g=G).rearrange(
            "p g (q o) -> p g q o", q=S)
        bias_nat = sb("bias_nat", [1, CO])
        ones = sb("ones", [1, N])
        p_col = sb("p_col", [P, 1])
        a_nat = sb("a_nat", [P, E, S * R])
        toep_nat = y[:, 0:2, :, :].rearrange("p c n j -> p c (n j)")
        w_slots = [x_keep[:, 1, 0, :], x_keep[:, 1, 1, :], zb[:, 0, :], zb[:, 1, :]]
        b_nat = sb("b_nat", [P, O])

        z_ps = ctx.enter_context(nc.psum_tensor("z_ps", [P, H, BANK], F32))
        m_ps = ctx.enter_context(nc.psum_tensor("m_ps", [P, H, BANK], F32))
        ring = [ctx.enter_context(nc.psum_tensor(f"ring{i}", [P, BANK], F32)) for i in range(3)]
        side = ctx.enter_context(nc.psum_tensor("side", [P, BANK], F32))
        w_banks = [z_ps[:, 0, :], z_ps[:, 1, :], m_ps[:, 0, :], m_ps[:, 1, :]]

        small_loaded, b_rows_loaded = sem("small_loaded"), sem("b_rows_loaded")
        a_loaded, b_loaded = sem("a_loaded"), sem("b_loaded")
        w_loaded = [sem(f"w_loaded{i}") for i in range(len(w_slots))]
        ident_zero, ident_ready, masks_ready = sem("ident_zero"), sem("ident_ready"), sem("masks_ready")
        consts_set, pads_zero = sem("consts_set"), sem("pads_zero")
        small_turned, small_copied = sem("small_turned"), sem("small_copied")
        shifts_ready, toep_loaded = sem("shifts_ready"), sem("toep_loaded")
        row_add_sum, toep_hi_ready, toep_ready = sem("row_add_sum"), sem("toep_hi_ready"), sem("toep_ready")
        w_turned, w_hi_ready, w_ready = sem("w_turned"), sem("w_hi_ready"), sem("w_ready")
        a_hi_ready, pb_scaled, pb_hi_ready, ab_ready = (
            sem(s) for s in ("a_hi_ready", "pb_scaled", "pb_hi_ready", "ab_ready"))
        t1_done, t2_done, edge_done, conv_done, t3_done = (
            sem(s) for s in ("t1_done", "t2_done", "edge_done", "conv_done", "t3_done"))
        u_done, z_done, m_done = sem("u_done"), sem("z_done"), sem("m_done")
        t1_copied, t2_hi, edge_hi, t3_hi, u_hi_ready = (
            sem(s) for s in ("t1_copied", "t2_hi", "edge_hi", "t3_hi", "u_hi_ready"))
        squared = sem("squared")
        edge_l_ready, t2_lo, edge_lo, conv_biased, t3_lo, u_lo_ready = (
            sem(s) for s in ("edge_l_ready", "t2_lo", "edge_lo", "conv_biased", "t3_lo", "u_lo_ready"))
        z_biased, gamma_steps, out_ready = sem("z_biased"), sem("gamma_steps"), sem("out_ready")
        z_free, m_free = sem("z_free"), sem("m_free")
        x_kept = sem("x_kept")
        x_added, norms_ready = sem("x_added"), sem("norms_ready")
        x_loaded = [sem(f"x_loaded{w}") for w in range(W2)]
        stored = [[sem(f"stored{s}{w}") for w in range(W2)] for s in range(2)]

        block = ctx.enter_context(nc.Block())

        def steps(engine, step):
            with engine.Fori(0, STEPS // 2 - 1) as pair:
                step(pair * 2 + 1, 1, pair + 1)
                step(pair * 2 + 2, 0, pair + 1)
            step(STEPS - 1, 1, STEPS // 2)

        @block.sync
        def _(sp):
            def load_x(tile, w):
                sp.dma_start(x_in[:, w, PAD:PAD + L],
                             x_tiles[bass.ds(tile, 1), :, :].rearrange("a p l -> (a p) l")
                             ).then_inc(x_loaded[w], 16)

            def snapped(value):
                return value if isinstance(value, int) else sp.snap(value)

            def load_w(ob):
                sp.dma_start(w_slots[ob % 4], ffn_w[ob * P:(ob + 1) * P, :]).then_inc(w_loaded[ob % 4], 16)

            for w in range(W2):
                sp.sem_inc(stored[1][w], 16)
            sp.dma_start(conv_nat[:, :], conv_w.rearrange("o i k -> o (i k)")).then_inc(small_loaded, 16)
            sp.dma_start(cond_nat[:, :], cond).then_inc(small_loaded, 16)
            sp.dma_start(cond_w_nat[:, :], cond_w).then_inc(small_loaded, 16)
            sp.dma_start(bias_nat[:, :], bias.rearrange("(a o) -> a o", a=1)).then_inc(small_loaded, 16)
            for e in range(E):
                sp.dma_start(p_col[e * R:(e + 1) * R, :],
                             p_scores[e:e + 1].rearrange("(a b) -> a b", a=1).partition_broadcast(R)
                             ).then_inc(small_loaded, 16)
            for w in range(W2):
                load_x(w, w)
            for ob in range(2):
                load_w(ob)
            sp.dma_start(a_nat[:, :, :], ffn_a.rearrange("e (j q) r -> j e (q r)", q=S)).then_inc(a_loaded, 16)
            sp.dma_start(b_nat[:, :], ffn_bm.rearrange("e r o -> (e r) o")).then_inc(b_loaded, 16)
            sp.dma_start(b_rows[:, :], ffn_b.rearrange("(a o) -> a o", a=1).partition_broadcast(P)
                         ).then_inc(b_rows_loaded, 16)
            sp.wait_ge(shifts_ready, 3)
            for s in range(S):
                for c in range(2):
                    m = 2 * S - 1 - S * c - s
                    sp.dma_start(toep_nat[s * CI:(s + 1) * CI, c, :],
                                 shifts[:, m:m + S, :].rearrange("i m o -> i (m o)")).then_inc(toep_loaded, 16)
            sp.wait_ge(toep_loaded, 16 * 2 * S)
            for ob in range(2, 4):
                load_w(ob)
            for ob in range(4, OB):
                sp.wait_ge(w_turned, 2 * (ob - 4) + 2)
                load_w(ob)

            def load_next(t):
                for w in range(W2):
                    tile, read, used = (snapped(v) for v in (W2 * t + W2 + w, 4 * t + 2 * w + 2, W2 * t + w + 1))
                    sp.wait_ge(t1_done, read)
                    sp.wait_ge(edge_l_ready, used)
                    sp.wait_ge(x_kept, used)
                    load_x(tile, w)

            def store(f, par, w):
                tile, whole = (snapped(v) for v in (W2 * f + w, W2 * f + w + 1))
                sp.wait_ge(out_ready, whole)
                sp.dma_start(out_tiles[bass.ds(tile, 1), :, :].rearrange("a p l -> (a p) l"),
                             x_keep[:, par, w, :]).then_inc(stored[par][w], 16)

            load_next(0)
            with sp.Fori(0, STEPS // 2 - 1) as pair:
                for par in (1, 0):
                    t = pair * 2 + (2 - par)
                    load_next(t)
                    for w in range(W2):
                        store(t - 1, 1 - par, w)
            for w in range(W2):
                store(STEPS - 2, 0, w)
            for w in range(W2):
                store(STEPS - 1, 1, w)
            for w in range(W2):
                sp.wait_ge(stored[0][w], 16 * (STEPS // 2))
                sp.wait_ge(stored[1][w], 16 * (STEPS // 2) + 16)

        @block.tensor
        def _(pe):
            def three(ps, pairs, first=True, last=True):
                for i, (lh, ll, rh, rl) in enumerate(pairs):
                    for k, (a, b) in enumerate(((lh, rh), (lh, rl), (ll, rh))):
                        mm = pe.matmul(ps, a, b, start=(first and i == 0 and k == 0),
                                       stop=(last and i == len(pairs) - 1 and k == 2))
                return mm

            def ring_free(use, t):
                if use >= 3:
                    kind, n = divmod(use - 3, 4)
                    pe.wait_ge((t1_copied, t2_lo, conv_biased, t3_lo)[kind], 4 * t + n + 1)
                elif not (isinstance(t, int) and t == 0):
                    pe.wait_ge(t3_lo, 4 * t - 4 + (4, 2, 3)[use])

            def t1(t, k):
                w, half_s = divmod(k, 2)
                bank = ring[k % 3]
                if half_s == 0:
                    pe.wait_ge(x_loaded[w], 16 * t + 16)
                ring_free(k, t)
                for a in range(4):
                    s = 4 * half_s + a
                    tr = pe.transpose(bank[:, a * P:(a + 1) * P], x_in[:, w, s:s + S * (J - 1) + 1:S],
                                      ident[:, :])
                tr.then_inc(t1_done, 1)

            def t2(t, n):
                bank = ring[(4 + n) % 3]
                pe.wait_ge(t1_copied, 4 * t + 2 * (n // NT) + 2)
                ring_free(4 + n, t)
                for g in range(G):
                    tr = pe.transpose(bank[:, g * P:(g + 1) * P],
                                      xT[:, n * G + g, :, :].rearrange("p s i -> p (s i)"), ident[:, :])
                tr.then_inc(t2_done, 1)

            def edge(t):
                pe.wait_ge(edge_l_ready, W2 * t + W2)
                if not (isinstance(t, int) and t == 0):
                    pe.wait_ge(u_lo_ready, t)
                for w in range(W2):
                    mm = pe.matmul(side[:, 256 + 8 * w:256 + 8 * w + 8],
                                   edge_l[:, w, :, :].rearrange("p s i -> p (s i)"), same_ng[:, :],
                                   start=True, stop=True)
                mm.then_inc(edge_done, 1)

            def conv(t, g):
                bank = ring[(8 + g) % 3]
                if g == 0:
                    pe.wait_ge(t2_lo, 4 * t + 4)
                    pe.wait_ge(edge_lo, t + 1)
                ring_free(8 + g, t)
                three(bank[:, :].rearrange("p (n j) -> p n j", n=NB),
                      [(toep_hi[:, g, c, :], toep_lo[:, g, c, :],
                        xs_hi[:, g, :, c:c + J], xs_lo[:, g, :, c:c + J]) for c in range(2)]
                      ).then_inc(conv_done, 1)

            def t3(t, g):
                bank = ring[(12 + g) % 3]
                pe.wait_ge(conv_biased, 4 * t + g + 1)
                ring_free(12 + g, t)
                for n in range(NB):
                    tr = pe.transpose(bank[:, n * P:(n + 1) * P], y[:, g, n, :], ident[:, :])
                tr.then_inc(t3_done, 1)

            def u(f, par):
                pe.wait_ge(t3_lo, 4 * f + 4)
                pe.wait_ge(edge_lo, f + 1)
                three(side[:, 0:W2 * P],
                      [(a_hi[:, q, :], a_lo[:, q, :], yT_hi[:, par, q, :], yT_lo[:, par, q, :])
                       for q in range(S)]).then_inc(u_done, 1)

            def z(f, par, w, h, part):
                if part == 0:
                    pe.wait_ge(z_free, 4 * f + 2 * w + h + 1)
                rows, cols = slice(w * P, (w + 1) * P), slice(h * BANK, (h + 1) * BANK)
                mm = three(z_ps[:, h, :],
                           [(yT_hi[:, par, q, rows], yT_lo[:, par, q, rows],
                             wt_hi[:, q, cols], wt_lo[:, q, cols]) for q in (2 * part, 2 * part + 1)],
                           first=(part == 0), last=(part == 3))
                if part == 3:
                    mm.then_inc(z_done, 1)

            def m(f, w):
                if w == 0:
                    pe.wait_ge(u_lo_ready, f + 1)
                pe.wait_ge(m_free, W2 * f + w + 1)
                rows = slice(w * P, (w + 1) * P)
                for h in range(H):
                    cols = slice(h * BANK, (h + 1) * BANK)
                    mm = three(m_ps[:, h, :],
                               [(u_hi[:, rows], u_lo[:, rows], pb_hi[:, cols], pb_lo[:, cols])])
                mm.then_inc(m_done, 1)

            pe.wait_ge(ident_ready, 1)
            pe.wait_ge(small_loaded, 16 * (4 + E))
            pe.transpose(side[:, 0:N], cond_nat[:, :], ident[0:N, 0:N])
            pe.transpose(side[:, N:N + CO], cond_w_nat[:, :], ident[0:CO, 0:CO]).then_inc(small_turned, 1)
            taps = conv_nat[:, :].rearrange("o (i k) -> o k i", k=K)
            for slot in range(K):
                bank, at = ring[slot // 8], slot % 8
                mm = pe.matmul(bank[0:CI, at * CO:(at + 1) * CO], taps[:, K - 1 - slot, :],
                               ident[0:CO, 0:CO], start=True, stop=True)
            mm.then_inc(small_turned, 1)
            pe.wait_ge(small_copied, 3)
            for g in range(G):
                pe.matmul(side[:, N * g:N * (g + 1)], cw_wide[:, g, :, :].rearrange("d q o -> d (q o)"),
                          condT[:, 0:N], start=True, stop=False)
                mm = pe.matmul(side[:, N * g:N * (g + 1)],
                               bias_wide[:, g, :, :].rearrange("d q o -> d (q o)"), ones[:, :],
                               start=False, stop=True)
            mm.then_inc(row_add_sum, 1)
            pe.wait_ge(shifts_ready, 3)
            pe.wait_ge(pads_zero, 1)
            for k in range(4):
                t1(0, k)
            for n in range(NB):
                t2(0, n)
            pe.wait_ge(masks_ready, 1)
            edge(0)

            def turn_w(ob, h):
                k = 2 * ob + h
                if h == 0:
                    pe.wait_ge(w_loaded[ob % 4], 16 * (ob // 4 + 1))
                if k >= 4:
                    pe.wait_ge(w_ready, k - 3)
                for a in range(4):
                    q = 4 * h + a
                    tr = pe.transpose(w_banks[k % 4][:, a * P:(a + 1) * P],
                                      w_slots[ob % 4][:, q:q + S * (J - 1) + 1:S], ident[:, :])
                tr.then_inc(w_turned, 1)

            for ob in range(2):
                for h in range(2):
                    turn_w(ob, h)
            pe.wait_ge(toep_ready, 2)
            for g in range(G):
                conv(0, g)
                turn_w(2 + g // 2, g % 2)
            for g in range(G):
                t3(0, g)
                turn_w(4 + g // 2, g % 2)
            for ob in range(6, OB):
                for h in range(2):
                    turn_w(ob, h)
            pe.wait_ge(w_ready, 2 * OB)
            pe.wait_ge(ab_ready, 2)

            def step(t, par, turn):
                f, fp = t - 1, 1 - par
                t1(t, 0)
                t1(t, 1)
                u(f, fp)
                z(f, fp, 0, 0, 0)
                t1(t, 2)
                z(f, fp, 0, 0, 1)
                t1(t, 3)
                z(f, fp, 0, 0, 2)
                t2(t, 0)
                z(f, fp, 0, 0, 3)
                t2(t, 1)
                z(f, fp, 0, 1, 0)
                t2(t, 2)
                z(f, fp, 0, 1, 1)
                t2(t, 3)
                edge(t)
                z(f, fp, 0, 1, 2)
                z(f, fp, 0, 1, 3)
                conv(t, 0)
                m(f, 0)
                conv(t, 1)
                z(f, fp, 1, 0, 0)
                conv(t, 2)
                z(f, fp, 1, 0, 1)
                conv(t, 3)
                z(f, fp, 1, 0, 2)
                t3(t, 0)
                z(f, fp, 1, 0, 3)
                t3(t, 1)
                z(f, fp, 1, 1, 0)
                t3(t, 2)
                z(f, fp, 1, 1, 1)
                t3(t, 3)
                z(f, fp, 1, 1, 2)
                z(f, fp, 1, 1, 3)
                m(f, 1)

            steps(pe, step)
            u(STEPS - 1, 1)
            for w in range(W2):
                for h in range(H):
                    for part in range(4):
                        z(STEPS - 1, 1, w, h, part)
                m(STEPS - 1, w)

        @block.scalar
        def _(act):
            def copy(dst, src):
                return act.activation(dst, src, ACT.Copy)

            def t1_copy(t, k):
                act.wait_ge(t1_done, 4 * t + k + 1)
                w, half_s = divmod(k, 2)
                tile = xT[:, NT * G * w:NT * G * (w + 1), 4 * half_s:4 * half_s + 4, :]
                copy(tile.rearrange("p a s i -> p s a i"),
                     ring[k % 3][:, :].rearrange("p (s a i) -> p s a i", s=4, i=CI)).then_inc(t1_copied, 1)

            def t2_high(t, n):
                act.wait_ge(t2_done, 4 * t + n + 1)
                copy(xs_hi[:, :, n, 0:J],
                     ring[(4 + n) % 3][:, :].rearrange("p (g j) -> p g j", g=G)).then_inc(t2_hi, 1)

            def edge_high(t):
                act.wait_ge(edge_done, t + 1)
                copy(xs_hi[:, :, :, J].rearrange("p g n -> p n g"),
                     side[:, 256:272].rearrange("p (n g) -> p n g", n=NB)).then_inc(edge_hi, 1)

            def t3_high(t, par, g):
                act.wait_ge(t3_done, 4 * t + g + 1)
                yv = yT_hi[:, par, :, :].rearrange("p q (n g o) -> p g n q o", n=NB, g=G)
                copy(yv[:, g, :, :, :],
                     ring[(12 + g) % 3][:, :].rearrange("p (n q o) -> p n q o", n=NB, q=S)).then_inc(t3_hi, 1)

            def u_high(f):
                act.wait_ge(u_done, f + 1)
                copy(u_hi[:, :], side[:, 0:W2 * P]).then_inc(u_hi_ready, 1)

            def square_z(f, w):
                act.wait_ge(z_biased, 4 * f + 2 * w + 2)
                act.activation(squares[:, :], zb[:, w, :], ACT.Square,
                               accum_out=ssq[:, w, 0:1]).then_inc(squared, 1)

            def square_m(f, w):
                act.wait_ge(squared, 4 * f + 2 * w + 1)
                act.wait_ge(m_done, W2 * f + w + 1)
                act.activation(squares[:, :], m_ps[:, :, :].rearrange("p h c -> p (h c)"), ACT.Square,
                               accum_out=ssq[:, w, 1:2]).then_inc(squared, 1)

            act.wait_ge(small_turned, 1)
            copy(condT[:, :], side[0:D, 0:N + CO]).then_inc(small_copied, 1)
            act.wait_ge(row_add_sum, 1)
            copy(row_add[:, :, :], side[:, 0:G * N].rearrange("p (g n) -> p g n", g=G)).then_inc(shifts_ready, 1)
            for k in range(4):
                t1_copy(0, k)
            for n in range(NB):
                t2_high(0, n)
            edge_high(0)

            def w_high(k):
                ob, h = divmod(k, 2)
                act.wait_ge(w_turned, k + 1)
                copy(wt_hi[:, 4 * h:4 * h + 4, ob * P:(ob + 1) * P],
                     w_banks[k % 4].rearrange("p (q o) -> p q o", q=4)).then_inc(w_hi_ready, 1)

            act.wait_ge(toep_loaded, 16 * 2 * S)
            for c in range(2):
                copy(toep_hi[:, :, c, :].rearrange("p g (q o) -> p g q o", q=S),
                     toep_nat[:, c, :].rearrange("p (q g o) -> p g q o", q=S, g=G)).then_inc(toep_hi_ready, 1)
            for k in range(2 * OB - 4):
                if k >= 8:
                    t3_high(0, 0, k - 8)
                w_high(k)
            for k in range(2 * OB - 4, 2 * OB):
                w_high(k)
            act.wait_ge(a_loaded, 16)
            copy(a_hi[:, :, :].rearrange("p q (e r) -> p q e r", e=E),
                 a_nat[:, :, :].rearrange("p e (q r) -> p q e r", q=S)).then_inc(a_hi_ready, 1)
            act.wait_ge(pb_scaled, 1)
            copy(pb_hi[:, :], b_nat[:, :]).then_inc(pb_hi_ready, 1)

            def step(t, par, turn):
                f = t - 1
                t1_copy(t, 0)
                t1_copy(t, 1)
                u_high(f)
                t1_copy(t, 2)
                t1_copy(t, 3)
                for n in range(NB):
                    t2_high(t, n)
                edge_high(t)
                square_z(f, 0)
                square_m(f, 0)
                for g in range(G):
                    t3_high(t, par, g)
                square_z(f, 1)
                square_m(f, 1)

            steps(act, step)
            u_high(STEPS - 1)
            for w in range(W2):
                square_z(STEPS - 1, w)
                square_m(STEPS - 1, w)

        @block.vector
        def _(dve):
            def rest(dst, whole, high):
                return dve.tensor_tensor(dst, whole, high.bitcast(F32), ALU.subtract)

            def edge_left(t, w):
                if not (isinstance(t, int) and t == 0):
                    dve.wait_ge(edge_done, t)
                dve.wait_ge(x_loaded[w], 16 * t + 16)
                dve.tensor_tensor(edge_l[:, w, :, :],
                                  x_in[:, w, L:L + S].unsqueeze(2).to_broadcast([P, S, CI]),
                                  same_i[:, :].unsqueeze(1).to_broadcast([P, S, CI]),
                                  ALU.mult).then_inc(edge_l_ready, 1)

            def keep_x(t, par, w, stores):
                dve.wait_ge(x_loaded[w], 16 * t + 16)
                if stores is not None:
                    dve.wait_ge(stored[par][w], 16 * stores)
                dve.tensor_copy(x_keep[:, par, w, :], x_in[:, w, PAD:PAD + L]).then_inc(x_kept, 1)

            def t2_low(t, n):
                dve.wait_ge(t2_hi, 4 * t + n + 1)
                rest(xs_lo[:, :, n, 0:J], ring[(4 + n) % 3][:, :].rearrange("p (g j) -> p g j", g=G),
                     xs_hi[:, :, n, 0:J]).then_inc(t2_lo, 1)

            def edge_low(t):
                dve.wait_ge(edge_hi, t + 1)
                rest(xs_lo[:, :, :, J].rearrange("p g n -> p n g"),
                     side[:, 256:272].rearrange("p (n g) -> p n g", n=NB),
                     xs_hi[:, :, :, J].rearrange("p g n -> p n g")).then_inc(edge_lo, 1)

            def conv_bias(t, g):
                dve.wait_ge(conv_done, 4 * t + g + 1)
                dve.tensor_tensor(y[:, g, :, :],
                                  ring[(8 + g) % 3][:, :].rearrange("p (n j) -> p n j", n=NB),
                                  row_add[:, g, bass.ds(t * NB, NB)].unsqueeze(2).to_broadcast([P, NB, J]),
                                  ALU.add).then_inc(conv_biased, 1)

            def t3_low(t, par, g):
                dve.wait_ge(t3_hi, 4 * t + g + 1)
                lo, hi = (v[:, par, :, :].rearrange("p q (n g o) -> p g n q o", n=NB, g=G)[:, g, :, :, :]
                          for v in (yT_lo, yT_hi))
                rest(lo, ring[(12 + g) % 3][:, :].rearrange("p (n q o) -> p n q o", n=NB, q=S),
                     hi).then_inc(t3_lo, 1)

            def u_low(f):
                dve.wait_ge(u_hi_ready, f + 1)
                rest(u_lo[:, :], side[:, 0:W2 * P], u_hi[:, :]).then_inc(u_lo_ready, 1)

            def z_bias(f, w, h):
                dve.wait_ge(z_done, 4 * f + 2 * w + h + 1)
                cols = slice(h * BANK, (h + 1) * BANK)
                dve.tensor_tensor(zb[:, w, cols], z_ps[:, h, :], b_rows[:, cols],
                                  ALU.add).then_inc(z_biased, 1)
                dve.wait_ge(z_biased, 4 * f + 2 * w + h + 1)
                dve.sem_inc(z_free, 1)

            def finish(f, par, w):
                tile = W2 * f + w
                dve.wait_ge(norms_ready, tile + 1)
                dve.tensor_scalar(den[:, w:w + 1], norms[:, w, 1:2], EPS, 1 / C_CLAMP,
                                  ALU.add, ALU.mult).then_inc(gamma_steps, 1)
                dve.wait_ge(gamma_steps, 3 * tile + 1)
                dve.reciprocal(rden[:, w:w + 1], den[:, w:w + 1]).then_inc(gamma_steps, 1)
                dve.wait_ge(gamma_steps, 3 * tile + 2)
                dve.tensor_scalar(gamma[:, w:w + 1], norms[:, w, 0:1], rden[:, w:w + 1], 1.0,
                                  ALU.mult, ALU.min).then_inc(gamma_steps, 1)
                dve.wait_ge(gamma_steps, 3 * tile + 3)
                dve.wait_ge(x_added, tile + 1)
                dve.scalar_tensor_tensor(x_keep[:, par, w, :], m_ps[:, :, :].rearrange("p h c -> p (h c)"),
                                         gamma[:, w:w + 1], x_keep[:, par, w, :],
                                         ALU.mult, ALU.add).then_inc(out_ready, 1)
                dve.wait_ge(out_ready, tile + 1)
                dve.sem_inc(m_free, 1)

            dve.sem_inc(z_free, 2)
            dve.sem_inc(m_free, 1)
            dve.memset(x_in[:, :, 0:PAD], 0.0)
            dve.memset(x_in[:, :, PAD + L:XP], 0.0)
            dve.memset(half[:, :], 0.5)
            dve.memset(ones[:, :], 1.0).then_inc(pads_zero, 1)
            dve.memset(shifts[:, :, :], 0.0).then_inc(consts_set, 1)
            dve.wait_ge(ident_ready, 1)
            dve.tensor_reduce(same_i[:, :], ident[:, :].rearrange("p (a i) -> p i a", i=CI), AX_X, ALU.add)
            dve.tensor_reduce(same_ng[:, :], ident[:, :].rearrange("p (a i) -> p a i", i=CI), AX_X,
                              ALU.add).then_inc(masks_ready, 1)
            dve.wait_ge(small_loaded, 16 * (4 + E))
            dve.tensor_copy(bias_wide[:, :, :, :],
                            bias_nat[:, :].rearrange("a (g o) -> a g o", g=G).unsqueeze(2)
                            .to_broadcast([1, G, S, OG])).then_inc(small_copied, 1)
            dve.wait_ge(small_copied, 2)
            dve.tensor_copy(cw_wide[:, :, :, :],
                            condT[:, N:N + CO].rearrange("d (g o) -> d g o", g=G).unsqueeze(2)
                            .to_broadcast([D, G, S, OG])).then_inc(small_copied, 1)
            dve.wait_ge(small_turned, 2)
            dve.wait_ge(consts_set, 1)
            dve.tensor_copy(shifts[:, S - 1:2 * S - 1, :],
                            ring[0][0:CI, :].rearrange("p (s o) -> p s o", s=8)).then_inc(shifts_ready, 1)
            dve.tensor_copy(shifts[:, 2 * S - 1, :], ring[1][0:CI, 0:CO]).then_inc(shifts_ready, 1)
            dve.wait_ge(masks_ready, 1)
            for w in range(W2):
                edge_left(0, w)
                keep_x(0, 0, w, None)
            for n in range(NB):
                t2_low(0, n)
            edge_low(0)
            for c in range(2):
                dve.wait_ge(toep_hi_ready, c + 1)
                rest(toep_lo[:, :, c, :].rearrange("p g (q o) -> p g q o", q=S),
                     toep_nat[:, c, :].rearrange("p (q g o) -> p g q o", q=S, g=G),
                     toep_hi[:, :, c, :].rearrange("p g (q o) -> p g q o", q=S)).then_inc(toep_ready, 1)

            def w_low(k):
                ob, h = divmod(k, 2)
                dve.wait_ge(w_hi_ready, k + 1)
                dst = (slice(None), slice(4 * h, 4 * h + 4), slice(ob * P, (ob + 1) * P))
                rest(wt_lo[dst], w_banks[k % 4].rearrange("p (q o) -> p q o", q=4),
                     wt_hi[dst]).then_inc(w_ready, 1)

            for k in range(4):
                w_low(k)
            dve.wait_ge(toep_ready, 2)
            for g in range(G):
                conv_bias(0, g)
                w_low(4 + g)
            for g in range(G):
                t3_low(0, 0, g)
                w_low(8 + g)
            for k in range(12, 2 * OB):
                w_low(k)
            dve.wait_ge(a_hi_ready, 1)
            rest(a_lo[:, :, :].rearrange("p q (e r) -> p q e r", e=E),
                 a_nat[:, :, :].rearrange("p e (q r) -> p q e r", q=S),
                 a_hi[:, :, :].rearrange("p q (e r) -> p q e r", e=E)).then_inc(ab_ready, 1)
            dve.wait_ge(b_loaded, 16)
            dve.tensor_scalar(b_nat[:, :], b_nat[:, :], p_col[:, :], None, ALU.mult).then_inc(pb_scaled, 1)
            dve.wait_ge(pb_hi_ready, 1)
            rest(pb_lo[:, :], b_nat[:, :], pb_hi[:, :]).then_inc(ab_ready, 1)
            dve.wait_ge(b_rows_loaded, 16)

            def step(t, par, turn):
                f = t - 1
                edge_left(t, 0)
                keep_x(t, par, 0, turn)
                u_low(f)
                edge_left(t, 1)
                t2_low(t, 0)
                keep_x(t, par, 1, turn)
                z_bias(f, 0, 0)
                for n in range(1, NB):
                    t2_low(t, n)
                edge_low(t)
                z_bias(f, 0, 1)
                conv_bias(t, 0)
                conv_bias(t, 1)
                conv_bias(t, 2)
                finish(f, 1 - par, 0)
                conv_bias(t, 3)
                t3_low(t, par, 0)
                z_bias(f, 1, 0)
                for g in range(1, G):
                    t3_low(t, par, g)
                z_bias(f, 1, 1)
                finish(f, 1 - par, 1)

            steps(dve, step)
            u_low(STEPS - 1)
            for w in range(W2):
                for h in range(H):
                    z_bias(STEPS - 1, w, h)
                finish(STEPS - 1, 1, w)

        @block.gpsimd
        def _(pool):
            def add_x(f, par, w):
                pool.wait_ge(z_biased, 4 * f + 2 * w + 2)
                pool.tensor_tensor(x_keep[:, par, w, :], x_keep[:, par, w, :], zb[:, w, :],
                                   ALU.add).then_inc(x_added, 1)

            def roots(f, w):
                pool.wait_ge(squared, 4 * f + 2 * w + 2)
                pool.tensor_tensor(norms[:, w, :], ssq[:, w, :], half[:, :], ALU.pow).then_inc(norms_ready, 1)

            pool.memset(ident[:, :], 0.0).then_inc(ident_zero, 1)
            pool.wait_ge(ident_zero, 1)
            pool.affine_select(out=ident[:, :], in_=ident[:, :], compare_op=ALU.not_equal, fill=1.0, base=0,
                               pattern=[[-1, P]], channel_multiplier=1).then_inc(ident_ready, 1)
            pool.wait_ge(pads_zero, 1)
            with pool.Fori(0, STEPS // 2 - 1) as pair:
                for par in (1, 0):
                    t = pair * 2 + (2 - par)
                    for w in range(W2):
                        add_x(t - 1, 1 - par, w)
                        roots(t - 1, w)
            for f, par in ((STEPS - 2, 0), (STEPS - 1, 1)):
                for w in range(W2):
                    add_x(f, par, w)
                    roots(f, w)


_INS = ["x", "cond_128", "fside_S_0", "L0_cond_weight", "L0_cond_c_weight", "L0_ffn_W", "L0_ffn_b",
        "L0_ffn_A", "L0_ffn_B", "L0_ffn_p_scores"]


def kernel(**inputs):
    import numpy as np
    import concourse.bacc as bacc
    from concourse.bass_utils import run_bass_kernel_spmd

    nc = bacc.Bacc("TRN2", target_bir_lowering=False, num_devices=1)
    arrays, args = {}, []
    for name in _INS:
        a = np.ascontiguousarray(inputs[name])
        arrays[f"in_{name}"] = a
        args.append(nc.dram_tensor(f"in_{name}", a.shape, mybir.dt.from_np(a.dtype), kind="ExternalInput").ap())
    shape = inputs["x"].shape
    out = nc.dram_tensor("out", shape, F32, kind="ExternalOutput").ap()
    build(nc, *args, out)
    r = run_bass_kernel_spmd(nc, [arrays], core_ids=[0])
    return r.results[0]["out"]
```

```python
from contextlib import ExitStack

import concourse.bass as bass
from concourse import mybir

F32 = mybir.dt.float32
F32R = mybir.dt.float32r
BF16 = mybir.dt.bfloat16
ALU = mybir.AluOpType
ACT = mybir.ActivationFunctionType
AX_X = mybir.AxisListType.X

P = 128
BANK = 512
C_CLAMP = 0.5
EPS = 1e-6


def build(nc, x, cond, bias, conv_w, cond_w, ffn_w, ffn_b, ffn_a, ffn_bm, p_scores, out):
    N, C, L = x.shape
    CO, CI, K = conv_w.shape
    G = C // CI
    OG = CO // G
    PAD = K // 2
    S = P // CI
    J = L // S
    D = cond.shape[1]
    O = ffn_w.shape[0]
    E, _, R = ffn_a.shape
    ER = E * R
    NB = 4
    W2 = NB * C // P
    NT = NB // W2
    STEPS = N // NB
    XP = L + PAD
    JE = J + 2
    OB = O // P
    H = O // BANK
    SLOTS = 2 * S + S - 1
    Q0 = S // 4
    JB = J // 32
    KT = JB * Q0
    assert KT == S and J == P and OG * S == P and ER == P and S == 2 * PAD and H == 2 and G == NB == 4

    x_tiles = x.rearrange("(t w n) c l -> (t w) (n c) l", w=W2, n=NT)
    out_tiles = out.rearrange("(t w n) c l -> (t w) (n c) l", w=W2, n=NT)

    with ExitStack() as ctx:
        def sb(name, shape, dt=F32):
            return ctx.enter_context(nc.sbuf_tensor(name, shape, dt))

        def sem(name):
            return ctx.enter_context(nc.semaphore(name))

        wt_hi, wt_lo = (sb(f"wt_{h}", [P, S, O], F32R) for h in ("hi", "lo"))
        a_hi, a_lo = (sb(f"a_{h}", [P, S, ER], F32R) for h in ("hi", "lo"))
        pb_hi, pb_lo = (sb(f"pb_{h}", [P, O], F32R) for h in ("hi", "lo"))
        toep_hi, toep_lo = (sb(f"toep_{h}", [P, G, 2, P], F32R) for h in ("hi", "lo"))
        row_add = sb("row_add", [P, G, N])
        b_rows = sb("b_rows", [P, O])
        x_in = sb("x_in", [P, W2, XP])
        x_keep = sb("x_keep", [P, 2, W2, L])
        xq = sb("xq", [P, W2 * L])
        xe = sb("xe", [P, W2 * L])
        xs_hi, xs_lo = (sb(f"xs_{h}", [P, NB, G, JE], F32R) for h in ("hi", "lo"))
        y = sb("y", [P, 2, NB, J])
        yt = sb("yt", [P, 2, NB, J])
        yT_hi, yT_lo = (sb(f"yT_{h}", [P, 2, KT, W2 * P], F32R) for h in ("hi", "lo"))
        u_hi, u_lo = (sb(f"u_{h}", [P, W2 * P], F32R) for h in ("hi", "lo"))
        zb = sb("zb", [P, W2, O])
        squares = sb("squares", [P, O // 2])
        ident = sb("ident", [P, P])
        half = sb("half", [P, 2])
        ssq = sb("ssq", [P, W2, 2])
        norms = sb("norms", [P, W2, 2])
        den = sb("den", [P, W2])
        rden = sb("rden", [P, W2])
        gamma = sb("gamma", [P, W2])
        conv_nat = xe[0:CO, 0:CI * K]
        w_pad = sb("w_pad", [CO, SLOTS, CI])
        cond_nat = xe[0:N, CI * K:CI * K + D]
        cond_w_nat = xe[0:CO, CI * K + D:CI * K + 2 * D]
        w_spare = sb("w_spare", [P, BANK])
        condT = sb("condT", [D, N + CO])
        bias_nat = sb("bias_nat", [1, CO])
        p_nat = sb("p_nat", [1, E])
        p_wide = sb("p_wide", [1, ER])
        ones = sb("ones", [1, N])
        p_col = sb("p_col", [P, 1])
        wide = yt[:, :, :, :].rearrange("p b n j -> p b (n j)").rearrange("p b (g q o) -> p b g q o", g=G, q=S)
        cw_wide, bias_wide = wide[:, 0, :, :, :], wide[0:1, 1, :, :, :]
        a_nat = y[:, :, :, :].rearrange("p c n j -> p (c n j)").rearrange("p (e q r) -> p e q r", e=E, q=S)
        b_nat = zb[:, 1, :]
        w_slots = [zb[:, 0, :], zb[:, 1, :], x_keep[:, 0, 0, :], x_keep[:, 0, 1, :],
                   x_keep[:, 1, 0, :], x_keep[:, 1, 1, :], b_rows[:, :]]
        w_sorted = [v.rearrange("p (k x) -> p k x", k=KT // 2)
                    for v in (w_spare[:, :], squares[:, :], yt[:, 0, :, :].rearrange("p n j -> p (n j)"),
                              yt[:, 1, :, :].rearrange("p n j -> p (n j)"))]

        z_ps = ctx.enter_context(nc.psum_tensor("z_ps", [P, H, BANK], F32))
        m_ps = ctx.enter_context(nc.psum_tensor("m_ps", [P, H, BANK], F32))
        conv_ps = [ctx.enter_context(nc.psum_tensor(f"conv_ps{i}", [P, BANK], F32)) for i in range(3)]
        side = ctx.enter_context(nc.psum_tensor("side", [P, BANK], F32))
        toep_ps, a_ps = conv_ps[0:2], [conv_ps[2], side]
        w_banks = [z_ps[:, 0, :], z_ps[:, 1, :], m_ps[:, 0, :], m_ps[:, 1, :]]

        small_loaded, b_rows_loaded = sem("small_loaded"), sem("b_rows_loaded")
        a_loaded, b_loaded = sem("a_loaded"), sem("b_loaded")
        w_loaded = [sem(f"w_loaded{i}") for i in range(OB)]
        ident_zero, ident_ready, w_pad_zero, w_pad_ready = (
            sem(s) for s in ("ident_zero", "ident_ready", "w_pad_zero", "w_pad_ready"))
        consts_set = sem("consts_set")
        cond_turned, cond_copied, widened, toep_placed, rows_summed, rows_copied = (
            sem(s) for s in ("cond_turned", "cond_copied", "widened", "toep_placed", "rows_summed", "rows_copied"))
        toep_hi_ready, toep_ready = sem("toep_hi_ready"), sem("toep_ready")
        pool_sorted, act_sorted, dve_sorted = sem("pool_sorted"), sem("act_sorted"), sem("dve_sorted")
        w_turned, w_hi_ready, w_ready = (sem(s) for s in ("w_turned", "w_hi_ready", "w_ready"))
        a_permuted, a_hi_ready, a_ready, pb_scaled, pb_hi_ready, pb_ready = (
            sem(s) for s in ("a_permuted", "a_hi_ready", "a_ready", "pb_scaled", "pb_hi_ready", "pb_ready"))
        conv_done, u_done, z_done, m_done = sem("conv_done"), sem("u_done"), sem("z_done"), sem("m_done")
        x_edge_hi, x_hi_ready, y_hi_ready, u_hi_ready, squared = (
            sem(s) for s in ("x_edge_hi", "x_hi_ready", "y_hi_ready", "u_hi_ready", "squared"))
        x_ended, x_turned, x_back, x_edge_lo, x_cleared = (
            sem(s) for s in ("x_ended", "x_turned", "x_back", "x_edge_lo", "x_cleared"))
        x_kept, x_lo_ready, conv_biased, y_turned, y_lo_ready, u_lo_ready = (
            sem(s) for s in ("x_kept", "x_lo_ready", "conv_biased", "y_turned", "y_lo_ready", "u_lo_ready"))
        z_biased, gamma_steps, out_ready = sem("z_biased"), sem("gamma_steps"), sem("out_ready")
        z_free, m_free = sem("z_free"), sem("m_free")
        x_added, norms_ready = sem("x_added"), sem("norms_ready")
        exchanged = sem("exchanged")
        x_loaded = [sem(f"x_loaded{w}") for w in range(W2)]
        stored = [[sem(f"stored{s}{w}") for w in range(W2)] for s in range(2)]

        block = ctx.enter_context(nc.Block())

        def steps(engine, step):
            with engine.Fori(0, STEPS // 2 - 1) as pair:
                step(pair * 2 + 1, 1, pair + 1)
                step(pair * 2 + 2, 0, pair + 1)
            step(STEPS - 1, 1, STEPS // 2)

        def is_last(t):
            return isinstance(t, int) and t == STEPS - 1

        def lower(v):
            return v[0:P // 2]

        def x_half(g0):
            return xq[:, :].rearrange("p (a jb g0 jf) -> p a g0 jb jf", jb=JB, g0=2, jf=32)[:, :, g0, :, :]

        x_column0 = lower(xq[:, :].rearrange("p (a jb g0 jf) -> p a g0 jb jf", jb=JB, g0=2, jf=32)[:, :, :, 0, 0])

        def xs_parts(v, g0):
            return v[:, :, :, 0:J].rearrange("p n (gp g0) (jb jf) -> p (n gp) g0 jb jf", g0=2, jf=32)[:, :, g0, :, :]

        def xs_last(v):
            return lower(v[:, :, :, J].rearrange("p n (gp g0) -> p (n gp) g0", g0=2))

        def toep_part(c, q0):
            hi, lo = (v[:, :, c, :].rearrange("p g (qq q0 o) -> p g qq q0 o", qq=4, q0=Q0)[:, :, :, q0, :]
                      for v in (toep_hi, toep_lo))
            nat = toep_ps[c][:, :].rearrange("p (q0 qq g o) -> p q0 g qq o", q0=Q0, qq=4, g=G)
            return hi, lo, nat[:, q0, :, :, :]

        POOL_SORTS, ACT_SORTS, DVE_SORTS = (1, 3, 5, 7, 9, 11, 13), (0, 4, 8, 12, 15), (2, 6, 10, 14)

        def sorted_by(k):
            for sorts, signal in ((POOL_SORTS, pool_sorted), (ACT_SORTS, act_sorted), (DVE_SORTS, dve_sorted)):
                if k in sorts:
                    return signal, sorts.index(k) + 1

        def sort_w(engine, copy, k):
            ob, h = divmod(k, 2)
            engine.wait_ge(w_loaded[ob], 16)
            if k in (2, 3):
                engine.wait_ge(rows_summed, 1)
            if k >= len(w_sorted):
                engine.wait_ge(w_turned, k - len(w_sorted) + 1)
            for a in range(2):
                jb = 2 * h + a
                part = w_slots[ob % len(w_slots)][:, jb * 32 * S:(jb + 1) * 32 * S].rearrange("p (jf q) -> p q jf", q=S)
                dst = w_sorted[k % len(w_sorted)][:, a * Q0:(a + 1) * Q0, :].rearrange(
                    "p k (qq jf) -> p (k qq) jf", qq=4)
                last = copy(dst, part)
            last.then_inc(sorted_by(k)[0], 1)

        @block.sync
        def _(sp):
            def load_x(tile, w):
                sp.dma_start(x_in[:, w, PAD:XP],
                             x_tiles[bass.ds(tile, 1), :, :].rearrange("a p l -> (a p) l")
                             ).then_inc(x_loaded[w], 16)

            def snapped(value):
                return value if isinstance(value, int) else sp.snap(value)

            def load_w(ob):
                sp.dma_start(w_slots[ob % len(w_slots)], ffn_w[ob * P:(ob + 1) * P, :]).then_inc(w_loaded[ob], 16)

            for w in range(W2):
                sp.sem_inc(stored[1][w], 16)
            for w in range(W2):
                load_x(w, w)
            sp.dma_start(conv_nat, conv_w.rearrange("o i k -> o (i k)")).then_inc(small_loaded, 16)
            sp.dma_start(cond_nat, cond).then_inc(small_loaded, 16)
            sp.dma_start(cond_w_nat, cond_w).then_inc(small_loaded, 16)
            sp.dma_start(bias_nat[:, :], bias.rearrange("(a o) -> a o", a=1)).then_inc(small_loaded, 16)
            sp.dma_start(p_nat[:, :], p_scores.rearrange("(a e) -> a e", a=1)).then_inc(small_loaded, 16)
            for ob in range(len(w_slots)):
                load_w(ob)
                if ob == OB // 2 - 1:
                    sp.dma_start(a_nat, ffn_a.rearrange("e (j q) r -> j e q r", q=S)).then_inc(a_loaded, 16)

            def load_next(t, w):
                tile, turned, kept = (snapped(v) for v in (W2 * t + W2 + w, 4 * t + 2 * w + 2, W2 * t + w + 1))
                sp.wait_ge(x_turned, turned)
                sp.wait_ge(x_kept, kept)
                load_x(tile, w)

            def exchange(t):
                first = isinstance(t, int) and t == 0
                turned, free = (snapped(v) for v in (4 * t + 4, t))
                sp.wait_ge(x_turned, turned)
                if not first:
                    sp.wait_ge(x_back, free)
                for a in range(4):
                    for b in range(4):
                        src = xq[32 * a:32 * a + 32, :].rearrange("p (w b x) -> p w b x", w=W2, b=4)
                        dst = xe[32 * b:32 * b + 32, :].rearrange("p (w a x) -> p w a x", w=W2, a=4)
                        sp.dma_start(dst[:, :, a, :], src[:, :, b, :]).then_inc(exchanged, 16)

            sp.wait_ge(cond_turned, 1)
            sp.wait_ge(w_pad_ready, 1)
            exchange(0)
            sp.wait_ge(w_turned, 2)
            load_w(OB - 1)
            for w in range(W2):
                load_next(0, w)
            sp.wait_ge(w_turned, 4)
            sp.dma_start(b_nat, ffn_bm.rearrange("e r o -> (e r) o")).then_inc(b_loaded, 16)
            sp.wait_ge(w_turned, 14)
            sp.dma_start(b_rows[:, :], ffn_b.rearrange("(a o) -> a o", a=1).partition_broadcast(P)
                         ).then_inc(b_rows_loaded, 16)

            def store(f, par, w):
                tile, whole = (snapped(v) for v in (W2 * f + w, W2 * f + w + 1))
                sp.wait_ge(out_ready, whole)
                sp.dma_start(out_tiles[bass.ds(tile, 1), :, :].rearrange("a p l -> (a p) l"),
                             x_keep[:, par, w, :]).then_inc(stored[par][w], 16)

            exchange(1)
            with sp.Fori(0, STEPS // 2 - 1) as pair:
                for par in (1, 0):
                    t = pair * 2 + (2 - par)
                    for w in range(W2):
                        load_next(t, w)
                    exchange(t + 1)
                    for w in range(W2):
                        store(t - 1, 1 - par, w)
            for w in range(W2):
                store(STEPS - 2, 0, w)
            for w in range(W2):
                store(STEPS - 1, 1, w)
            for w in range(W2):
                sp.wait_ge(stored[0][w], 16 * (STEPS // 2))
                sp.wait_ge(stored[1][w], 16 * (STEPS // 2) + 16)

        @block.tensor
        def _(pe):
            def three(ps, pairs, first=True, last=True):
                for i, (lh, ll, rh, rl) in enumerate(pairs):
                    for k, (a, b) in enumerate(((lh, rh), (lh, rl), (ll, rh))):
                        mm = pe.matmul(ps, a, b, start=(first and i == 0 and k == 0),
                                       stop=(last and i == len(pairs) - 1 and k == 2))
                return mm

            def conv(t, g):
                first = isinstance(t, int) and t == 0
                if g == 0:
                    pe.wait_ge(x_lo_ready, W2 * t + W2)
                if g == 3:
                    pe.wait_ge(conv_biased, 4 * t + 1)
                elif not first:
                    pe.wait_ge(conv_biased, 4 * t - 4 + (4, 2, 3)[g])
                three(conv_ps[g % 3][:, :].rearrange("p (n j) -> p n j", n=NB),
                      [(toep_hi[:, g, c, :], toep_lo[:, g, c, :],
                        xs_hi[:, :, g, c:c + J], xs_lo[:, :, g, c:c + J]) for c in range(2)]
                      ).then_inc(conv_done, 1)

            def u(f, par):
                pe.wait_ge(y_lo_ready, 4 * f + 4)
                three(side[:, 0:W2 * P],
                      [(a_hi[:, q, :], a_lo[:, q, :], yT_hi[:, par, q, :], yT_lo[:, par, q, :])
                       for q in range(KT)]).then_inc(u_done, 1)

            def z(f, par, w, h, part):
                if part == 0:
                    pe.wait_ge(z_free, 4 * f + 2 * w + h + 1)
                rows, cols = slice(w * P, (w + 1) * P), slice(h * BANK, (h + 1) * BANK)
                mm = three(z_ps[:, h, :],
                           [(yT_hi[:, par, q, rows], yT_lo[:, par, q, rows],
                             wt_hi[:, q, cols], wt_lo[:, q, cols]) for q in (2 * part, 2 * part + 1)],
                           first=(part == 0), last=(part == 3))
                if part == 3:
                    mm.then_inc(z_done, 1)

            def m(f, w):
                if w == 0:
                    pe.wait_ge(u_lo_ready, f + 1)
                pe.wait_ge(m_free, W2 * f + w + 1)
                rows = slice(w * P, (w + 1) * P)
                for h in range(H):
                    cols = slice(h * BANK, (h + 1) * BANK)
                    mm = three(m_ps[:, h, :],
                               [(u_hi[:, rows], u_lo[:, rows], pb_hi[:, cols], pb_lo[:, cols])])
                mm.then_inc(m_done, 1)

            pe.wait_ge(ident_ready, 1)
            pe.wait_ge(small_loaded, 16 * 5)
            pe.transpose(side[:, 0:N], cond_nat, ident[0:N, 0:N])
            pe.transpose(side[:, N:N + CO], cond_w_nat, ident[0:CO, 0:CO]).then_inc(cond_turned, 1)
            pe.wait_ge(w_pad_ready, 1)
            for c in range(2):
                for q in range(S):
                    first = S * c + S - 1 - q
                    mm = pe.matmul(toep_ps[c][:, q * CO:(q + 1) * CO],
                                   w_pad[:, first:first + S, :].rearrange("o k i -> o (k i)"),
                                   ident[0:CO, 0:CO], start=True, stop=True)
            mm.then_inc(toep_placed, 1)
            pe.wait_ge(cond_copied, 1)
            pe.wait_ge(widened, 3)
            for g in range(G):
                pe.matmul(side[:, N * g:N * (g + 1)], cw_wide[:, g, :, :].rearrange("d q o -> d (q o)"),
                          condT[:, 0:N], start=True, stop=False)
                pe.matmul(side[:, N * g:N * (g + 1)],
                          bias_wide[:, g, :, :].rearrange("d q o -> d (q o)"), ones[:, :],
                          start=False, stop=True)
            pe.matmul(a_ps[0][:, 0:2], p_wide[:, :], ones[:, 0:2], start=True, stop=True).then_inc(rows_summed, 1)

            def permute_a(part):
                for jb in (2 * part, 2 * part + 1):
                    for q0 in range(Q0):
                        kt = jb * Q0 + q0
                        cols = slice(kt % 4 * ER, (kt % 4 + 1) * ER)
                        for qq in range(4):
                            mm = pe.matmul(a_ps[part][32 * qq:32 * qq + 32, cols], ident[:, 32 * jb:32 * jb + 32],
                                           a_nat[:, :, 4 * q0 + qq, :], start=True, stop=True)
                mm.then_inc(a_permuted, 1)

            def turn_w(k):
                pe.wait_ge(*sorted_by(k))
                if k >= 4:
                    pe.wait_ge(w_ready, k - 3)
                for a in range(4):
                    tr = pe.transpose(w_banks[k % 4][:, a * P:(a + 1) * P], w_sorted[k % len(w_sorted)][:, a, :],
                                      ident[:, :])
                tr.then_inc(w_turned, 1)

            for k in range(8):
                turn_w(k)
            pe.wait_ge(a_loaded, 16)
            pe.wait_ge(rows_copied, 1)
            for part in range(2):
                permute_a(part)
            for k in range(8, 14):
                turn_w(k)
            pe.wait_ge(toep_ready, 1)
            pe.wait_ge(a_ready, 2)
            for g in range(G):
                conv(0, g)
                if g in (0, 1):
                    turn_w(14 + g)
            pe.wait_ge(w_ready, 2 * OB)
            pe.wait_ge(pb_ready, 1)

            def step(t, par, turn):
                f, fp = t - 1, 1 - par
                u(f, fp)
                for part in range(4):
                    z(f, fp, 0, 0, part)
                for part in range(3):
                    z(f, fp, 0, 1, part)
                conv(t, 0)
                z(f, fp, 0, 1, 3)
                m(f, 0)
                conv(t, 1)
                z(f, fp, 1, 0, 0)
                conv(t, 2)
                z(f, fp, 1, 0, 1)
                conv(t, 3)
                for part in range(2, 4):
                    z(f, fp, 1, 0, part)
                for part in range(4):
                    z(f, fp, 1, 1, part)
                m(f, 1)

            steps(pe, step)
            u(STEPS - 1, 1)
            for w in range(W2):
                for h in range(H):
                    for part in range(4):
                        z(STEPS - 1, 1, w, h, part)
                m(STEPS - 1, w)

        @block.scalar
        def _(act):
            def copy(dst, src):
                return act.activation(dst, src, ACT.Copy)

            def x_edge_high(t):
                act.wait_ge(x_back, t + 1)
                if not (isinstance(t, int) and t == 0):
                    act.wait_ge(conv_done, 4 * t)
                copy(xs_last(xs_hi), x_column0).then_inc(x_edge_hi, 1)

            def x_high(t, g0):
                act.wait_ge(x_cleared, t + 1)
                copy(xs_parts(xs_hi, g0), x_half(g0)).then_inc(x_hi_ready, 1)

            def y_high(t, par, g):
                act.wait_ge(y_turned, 4 * t + g + 1)
                yv = yT_hi[:, par, :, :].rearrange("p k (n g o) -> p g n k o", n=NB, g=G)
                copy(yv[:, g, :, :, :],
                     yt[:, g % 2, :, :].rearrange("p n (k o) -> p n k o", k=KT)).then_inc(y_hi_ready, 1)

            def u_high(f):
                act.wait_ge(u_done, f + 1)
                copy(u_hi[:, :], side[:, 0:W2 * P]).then_inc(u_hi_ready, 1)

            def square_z(f, w):
                act.wait_ge(z_biased, 4 * f + 2 * w + 2)
                act.activation(squares[:, :].bitcast(BF16), zb[:, w, :], ACT.Square,
                               accum_out=ssq[:, w, 0:1]).then_inc(squared, 1)

            def square_m(f, w):
                act.wait_ge(squared, 4 * f + 2 * w + 1)
                act.wait_ge(m_done, W2 * f + w + 1)
                act.activation(squares[:, :].bitcast(BF16), m_ps[:, :, :].rearrange("p h c -> p (h c)"), ACT.Square,
                               accum_out=ssq[:, w, 1:2]).then_inc(squared, 1)

            def w_high(k):
                ob, h = divmod(k, 2)
                act.wait_ge(w_turned, k + 1)
                copy(wt_hi[:, 4 * h:4 * h + 4, ob * P:(ob + 1) * P],
                     w_banks[k % 4].rearrange("p (q o) -> p q o", q=4)).then_inc(w_hi_ready, 1)

            def sort(k):
                sort_w(act, copy, k)

            def a_high(part):
                act.wait_ge(a_permuted, part + 1)
                copy(a_hi[:, 4 * part:4 * part + 4, :],
                     a_ps[part][:, :].rearrange("p (k x) -> p k x", x=ER)).then_inc(a_hi_ready, 1)

            act.wait_ge(cond_turned, 1)
            copy(condT[:, :], side[0:D, 0:N + CO]).then_inc(cond_copied, 1)
            act.wait_ge(toep_placed, 1)
            for c, q0 in ((c, q0) for c in range(2) for q0 in range(Q0)):
                hi, _, nat = toep_part(c, q0)
                last = copy(hi, nat)
            last.then_inc(toep_hi_ready, 1)
            sort(0)
            act.wait_ge(rows_summed, 1)
            copy(row_add[:, :, :], side[:, 0:G * N].rearrange("p (g n) -> p g n", g=G))
            copy(p_col[:, :], a_ps[0][:, 0:1]).then_inc(rows_copied, 1)
            for k in range(3):
                w_high(k)
            sort(4)
            for k in range(3, 6):
                w_high(k)
            sort(8)
            for k in range(6, 8):
                w_high(k)
            for part in range(2):
                a_high(part)
            w_high(8)
            sort(12)
            for k in range(9, 13):
                w_high(k)
            sort(15)
            w_high(13)
            x_edge_high(0)
            for g0 in range(2):
                x_high(0, g0)
            for k in (14, 15):
                w_high(k)
            act.wait_ge(pb_scaled, 1)
            copy(pb_hi[:, :], b_nat).then_inc(pb_hi_ready, 1)
            for g in range(G):
                y_high(0, 0, g)
            x_edge_high(1)
            for g0 in range(2):
                x_high(1, g0)

            def step(t, par, turn):
                f = t - 1
                u_high(f)
                square_z(f, 0)
                y_high(t, par, 0)
                square_m(f, 0)
                for g in range(1, G):
                    y_high(t, par, g)
                square_z(f, 1)
                square_m(f, 1)
                if not is_last(t):
                    x_edge_high(t + 1)
                    for g0 in range(2):
                        x_high(t + 1, g0)

            steps(act, step)
            u_high(STEPS - 1)
            for w in range(W2):
                square_z(STEPS - 1, w)
                square_m(STEPS - 1, w)

        @block.vector
        def _(dve):
            def rest(dst, whole, high):
                return dve.tensor_tensor(dst, whole, high.bitcast(F32), ALU.subtract)

            def keep_x(t, par, w, stores):
                dve.wait_ge(x_loaded[w], 16 * t + 16)
                if stores is not None:
                    dve.wait_ge(stored[par][w], 16 * stores)
                dve.tensor_copy(x_keep[:, par, w, :], x_in[:, w, PAD:XP]).then_inc(x_kept, 1)

            def turn_x(t):
                first = isinstance(t, int) and t == 0
                for w in range(W2):
                    dve.wait_ge(x_loaded[w], 16 * t + 16)
                dve.tensor_copy(x_in[:, :, 0:PAD], x_in[:, :, L:XP]).then_inc(x_ended, 1)
                dve.wait_ge(x_ended, t + 1)
                if not first:
                    dve.wait_ge(x_lo_ready, 2 * t)
                for w in range(W2):
                    rows = x_in[:, w, 0:L].rearrange("p (jb jf sp s0) -> p s0 sp jb jf", jf=32, sp=4, s0=2)
                    turned = xq[:, w * L:(w + 1) * L].rearrange("p (b g0 s0 i) -> p s0 b g0 i", g0=2, s0=2, i=CI)
                    for s0 in range(2):
                        dve.transpose(turned[:, s0, :, :, :], rows[:, s0, :, :, :]).then_inc(x_turned, 1)

            def turn_back(t):
                dve.wait_ge(exchanged, 256 * t + 256)
                dve.transpose(xq[:, :], xe[:, :]).then_inc(x_back, 1)

            def x_edge_low(t):
                dve.wait_ge(x_edge_hi, t + 1)
                rest(xs_last(xs_lo), x_column0, xs_last(xs_hi)).then_inc(x_edge_lo, 1)
                dve.wait_ge(x_edge_lo, t + 1)
                dve.memset(x_column0, 0.0).then_inc(x_cleared, 1)

            def x_low(t, g0):
                dve.wait_ge(x_hi_ready, 2 * t + g0 + 1)
                rest(xs_parts(xs_lo, g0), x_half(g0), xs_parts(xs_hi, g0)).then_inc(x_lo_ready, 1)

            def conv_bias(t, g):
                first = isinstance(t, int) and t == 0
                dve.wait_ge(conv_done, 4 * t + g + 1)
                if not first or g >= 2:
                    dve.wait_ge(y_turned, 4 * t + g - 1)
                dve.tensor_tensor(y[:, g % 2, :, :],
                                  conv_ps[g % 3][:, :].rearrange("p (n j) -> p n j", n=NB),
                                  row_add[:, g, bass.ds(t * NB, NB)].unsqueeze(2).to_broadcast([P, NB, J]),
                                  ALU.add).then_inc(conv_biased, 1)

            def turn_y(t, g):
                first = isinstance(t, int) and t == 0
                dve.wait_ge(conv_biased, 4 * t + g + 1)
                if not first or g >= 2:
                    dve.wait_ge(y_lo_ready, 4 * t + g - 1)
                dve.transpose(yt[:, g % 2, :, :].rearrange("p n j -> p (n j)"),
                              y[:, g % 2, :, :].rearrange("p n j -> p (n j)")).then_inc(y_turned, 1)

            def y_low(t, par, g):
                dve.wait_ge(y_hi_ready, 4 * t + g + 1)
                lo, hi = (v[:, par, :, :].rearrange("p k (n g o) -> p g n k o", n=NB, g=G)[:, g, :, :, :]
                          for v in (yT_lo, yT_hi))
                rest(lo, yt[:, g % 2, :, :].rearrange("p n (k o) -> p n k o", k=KT), hi).then_inc(y_lo_ready, 1)

            def u_low(f):
                dve.wait_ge(u_hi_ready, f + 1)
                rest(u_lo[:, :], side[:, 0:W2 * P], u_hi[:, :]).then_inc(u_lo_ready, 1)

            def z_bias(f, w, h):
                dve.wait_ge(z_done, 4 * f + 2 * w + h + 1)
                cols = slice(h * BANK, (h + 1) * BANK)
                dve.tensor_tensor(zb[:, w, cols], z_ps[:, h, :], b_rows[:, cols],
                                  ALU.add).then_inc(z_biased, 1)
                dve.wait_ge(z_biased, 4 * f + 2 * w + h + 1)
                dve.sem_inc(z_free, 1)

            def finish(f, par, w):
                tile = W2 * f + w
                dve.wait_ge(norms_ready, tile + 1)
                dve.tensor_scalar(den[:, w:w + 1], norms[:, w, 1:2], EPS, 1 / C_CLAMP,
                                  ALU.add, ALU.mult).then_inc(gamma_steps, 1)
                dve.wait_ge(gamma_steps, 3 * tile + 1)
                dve.reciprocal(rden[:, w:w + 1], den[:, w:w + 1]).then_inc(gamma_steps, 1)
                dve.wait_ge(gamma_steps, 3 * tile + 2)
                dve.tensor_scalar(gamma[:, w:w + 1], norms[:, w, 0:1], rden[:, w:w + 1], 1.0,
                                  ALU.mult, ALU.min).then_inc(gamma_steps, 1)
                dve.wait_ge(gamma_steps, 3 * tile + 3)
                dve.wait_ge(x_added, tile + 1)
                dve.scalar_tensor_tensor(x_keep[:, par, w, :], m_ps[:, :, :].rearrange("p h c -> p (h c)"),
                                         gamma[:, w:w + 1], x_keep[:, par, w, :],
                                         ALU.mult, ALU.add).then_inc(out_ready, 1)
                dve.wait_ge(out_ready, tile + 1)
                dve.sem_inc(m_free, 1)

            dve.sem_inc(z_free, 2)
            dve.sem_inc(m_free, 1)
            dve.memset(xs_hi[P // 2:P, :, :, J].bitcast(F32), 0.0)
            dve.memset(xs_lo[P // 2:P, :, :, J].bitcast(F32), 0.0)
            dve.memset(half[:, :], 0.5)
            dve.memset(ones[:, :], 1.0).then_inc(consts_set, 1)
            turn_x(0)
            dve.wait_ge(small_loaded, 16 * 5)
            dve.wait_ge(w_pad_zero, 1)
            dve.tensor_copy(w_pad[:, S - 1:S - 1 + K, :],
                            conv_nat.rearrange("o (i k) -> o k i", k=K)).then_inc(w_pad_ready, 1)
            dve.tensor_copy(bias_wide[:, :, :, :],
                            bias_nat[:, :].rearrange("a (g o) -> a g o", g=G).unsqueeze(2)
                            .to_broadcast([1, G, S, OG])).then_inc(widened, 1)
            dve.tensor_copy(p_wide[:, :].rearrange("a (e r) -> a e r", e=E),
                            p_nat[:, :].unsqueeze(2).to_broadcast([1, E, R])).then_inc(widened, 1)
            dve.wait_ge(cond_copied, 1)
            dve.tensor_copy(cw_wide[:, :, :, :],
                            condT[:, N:N + CO].rearrange("d (g o) -> d g o", g=G).unsqueeze(2)
                            .to_broadcast([D, G, S, OG])).then_inc(widened, 1)

            def w_low(k):
                ob, h = divmod(k, 2)
                dve.wait_ge(w_hi_ready, k + 1)
                dst = (slice(None), slice(4 * h, 4 * h + 4), slice(ob * P, (ob + 1) * P))
                rest(wt_lo[dst], w_banks[k % 4].rearrange("p (q o) -> p q o", q=4),
                     wt_hi[dst]).then_inc(w_ready, 1)

            def sort(k):
                sort_w(dve, dve.tensor_copy, k)

            def a_low(part):
                dve.wait_ge(a_hi_ready, part + 1)
                cols = (slice(None), slice(4 * part, 4 * part + 4))
                rest(a_lo[cols], a_ps[part][:, :].rearrange("p (k x) -> p k x", x=ER), a_hi[cols]
                     ).then_inc(a_ready, 1)

            dve.wait_ge(toep_hi_ready, 1)
            for c, q0 in ((c, q0) for c in range(2) for q0 in range(Q0)):
                hi, lo, nat = toep_part(c, q0)
                last = rest(lo, nat, hi)
            last.then_inc(toep_ready, 1)
            sort(2)
            for k in range(3):
                w_low(k)
            sort(6)
            for k in range(3, 6):
                w_low(k)
            sort(10)
            for k in range(6, 8):
                w_low(k)
            for w in range(W2):
                keep_x(0, 0, w, None)
            for part in range(2):
                a_low(part)
            for k in range(8, 12):
                w_low(k)
            sort(14)
            turn_back(0)
            for k in (12, 13):
                w_low(k)
            x_edge_low(0)
            for g0 in range(2):
                x_low(0, g0)
            for k in (14, 15):
                w_low(k)
            dve.wait_ge(b_loaded, 16)
            dve.tensor_scalar(b_nat, b_nat, p_col[:, :], None, ALU.mult).then_inc(pb_scaled, 1)
            for g in range(G):
                conv_bias(0, g)
                turn_y(0, g)
                if g == 0:
                    turn_x(1)
                    dve.wait_ge(pb_hi_ready, 1)
                    rest(pb_lo[:, :], b_nat, pb_hi[:, :]).then_inc(pb_ready, 1)
                y_low(0, 0, g)
            dve.wait_ge(b_rows_loaded, 16)
            turn_back(1)
            x_edge_low(1)
            for g0 in range(2):
                x_low(1, g0)

            def step(t, par, turn):
                f = t - 1
                for w in range(W2):
                    keep_x(t, par, w, turn)
                u_low(f)
                z_bias(f, 0, 0)
                if not is_last(t):
                    turn_x(t + 1)
                conv_bias(t, 0)
                turn_y(t, 0)
                z_bias(f, 0, 1)
                y_low(t, par, 0)
                conv_bias(t, 1)
                turn_y(t, 1)
                y_low(t, par, 1)
                conv_bias(t, 2)
                turn_y(t, 2)
                y_low(t, par, 2)
                conv_bias(t, 3)
                turn_y(t, 3)
                y_low(t, par, 3)
                finish(f, 1 - par, 0)
                z_bias(f, 1, 0)
                z_bias(f, 1, 1)
                if not is_last(t):
                    turn_back(t + 1)
                    x_edge_low(t + 1)
                finish(f, 1 - par, 1)
                if not is_last(t):
                    for g0 in range(2):
                        x_low(t + 1, g0)

            steps(dve, step)
            u_low(STEPS - 1)
            for w in range(W2):
                for h in range(H):
                    z_bias(STEPS - 1, w, h)
                finish(STEPS - 1, 1, w)

        @block.gpsimd
        def _(pool):
            def add_x(f, par, w):
                pool.wait_ge(z_biased, 4 * f + 2 * w + 2)
                pool.tensor_tensor(x_keep[:, par, w, :], x_keep[:, par, w, :], zb[:, w, :],
                                   ALU.add).then_inc(x_added, 1)

            def roots(f, w):
                pool.wait_ge(squared, 4 * f + 2 * w + 2)
                pool.tensor_tensor(norms[:, w, :], ssq[:, w, :], half[:, :], ALU.pow).then_inc(norms_ready, 1)

            pool.memset(w_pad[:, :, :], 0.0).then_inc(w_pad_zero, 1)
            pool.memset(ident[:, :], 0.0).then_inc(ident_zero, 1)
            pool.wait_ge(ident_zero, 1)
            pool.affine_select(out=ident[:, :], in_=ident[:, :], compare_op=ALU.not_equal, fill=1.0, base=0,
                               pattern=[[-1, P]], channel_multiplier=1).then_inc(ident_ready, 1)
            for k in POOL_SORTS:
                sort_w(pool, pool.tensor_copy, k)
            pool.wait_ge(consts_set, 1)
            with pool.Fori(0, STEPS // 2 - 1) as pair:
                for par in (1, 0):
                    t = pair * 2 + (2 - par)
                    for w in range(W2):
                        add_x(t - 1, 1 - par, w)
                        roots(t - 1, w)
            for f, par in ((STEPS - 2, 0), (STEPS - 1, 1)):
                for w in range(W2):
                    add_x(f, par, w)
                    roots(f, w)


_INS = ["x", "cond_128", "fside_S_0", "L0_cond_weight", "L0_cond_c_weight", "L0_ffn_W", "L0_ffn_b",
        "L0_ffn_A", "L0_ffn_B", "L0_ffn_p_scores"]


def kernel(**inputs):
    import numpy as np
    import concourse.bacc as bacc
    from concourse.bass_utils import run_bass_kernel_spmd

    nc = bacc.Bacc("TRN2", target_bir_lowering=False, num_devices=1)
    arrays, args = {}, []
    for name in _INS:
        a = np.ascontiguousarray(inputs[name])
        arrays[f"in_{name}"] = a
        args.append(nc.dram_tensor(f"in_{name}", a.shape, mybir.dt.from_np(a.dtype), kind="ExternalInput").ap())
    shape = inputs["x"].shape
    out = nc.dram_tensor("out", shape, F32, kind="ExternalOutput").ap()
    build(nc, *args, out)
    r = run_bass_kernel_spmd(nc, [arrays], core_ids=[0])
    return r.results[0]["out"]
```

```python
from contextlib import ExitStack

import concourse.bass as bass
from concourse import mybir

F32 = mybir.dt.float32
F32R = mybir.dt.float32r
BF16 = mybir.dt.bfloat16
ALU = mybir.AluOpType
ACT = mybir.ActivationFunctionType
AX_X = mybir.AxisListType.X

P = 128
BANK = 512
C_CLAMP = 0.5
EPS = 1e-6


def build(nc, x, cond, bias, conv_w, cond_w, ffn_w, ffn_b, ffn_a, ffn_bm, p_scores, out):
    N, C, L = x.shape
    CO, CI, K = conv_w.shape
    G = C // CI
    OG = CO // G
    PAD = K // 2
    S = P // CI
    J = L // S
    D = cond.shape[1]
    O = ffn_w.shape[0]
    E, _, R = ffn_a.shape
    ER = E * R
    NB = 4
    W2 = NB * C // P
    NT = NB // W2
    STEPS = N // NB
    XP = L + PAD
    JE = J + 2
    OB = O // P
    H = O // BANK
    SLOTS = 2 * S + S - 1
    Q0 = S // 4
    JB = J // 32
    KT = JB * Q0
    assert KT == S and J == P and OG * S == P and ER == P and S == 2 * PAD and H == 2 and G == NB == 4

    x_tiles = x.rearrange("(t w n) c l -> (t w) (n c) l", w=W2, n=NT)
    out_tiles = out.rearrange("(t w n) c l -> (t w) (n c) l", w=W2, n=NT)

    with ExitStack() as ctx:
        def sb(name, shape, dt=F32):
            return ctx.enter_context(nc.sbuf_tensor(name, shape, dt))

        def sem(name):
            return ctx.enter_context(nc.semaphore(name))

        wt_hi, wt_lo = (sb(f"wt_{h}", [P, S, O], F32R) for h in ("hi", "lo"))
        a_hi, a_lo = (sb(f"a_{h}", [P, S, ER], F32R) for h in ("hi", "lo"))
        pb_hi, pb_lo = (sb(f"pb_{h}", [P, O], F32R) for h in ("hi", "lo"))
        toep_hi, toep_lo = (sb(f"toep_{h}", [P, G, 2, P], F32R) for h in ("hi", "lo"))
        row_add = sb("row_add", [P, G, N])
        b_rows = sb("b_rows", [P, O])
        x_in = sb("x_in", [P, W2, XP])
        x_keep = sb("x_keep", [P, 2, W2, L])
        xq = sb("xq", [P, W2 * L])
        xe = sb("xe", [P, W2 * L])
        xs_hi, xs_lo = (sb(f"xs_{h}", [P, NB, G, JE], F32R) for h in ("hi", "lo"))
        y = sb("y", [P, 2, NB, J])
        yt = sb("yt", [P, 2, NB, J])
        yT_hi, yT_lo = (sb(f"yT_{h}", [P, 2, KT, W2 * P], F32R) for h in ("hi", "lo"))
        u_hi, u_lo = (sb(f"u_{h}", [P, W2 * P], F32R) for h in ("hi", "lo"))
        zb = sb("zb", [P, W2, O])
        squares = sb("squares", [P, O // 2])
        ident = sb("ident", [P, P])
        half = sb("half", [P, 2])
        ssq = sb("ssq", [P, W2, 2])
        ssq_half = sb("ssq_half", [P, 1])
        norms = sb("norms", [P, W2, 2])
        den = sb("den", [P, W2])
        rden = sb("rden", [P, W2])
        gamma = sb("gamma", [P, W2])
        conv_nat = x_keep[0:CO, 1, 1, 0:CI * K]
        w_pad = sb("w_pad", [CO, SLOTS, CI])
        cond_nat = x_keep[0:N, 1, 1, CI * K:CI * K + D]
        cond_w_nat = x_keep[0:CO, 1, 1, CI * K + D:CI * K + 2 * D]
        w_spare = sb("w_spare", [P, BANK])
        condT = sb("condT", [D, N + CO])
        bias_nat = sb("bias_nat", [1, CO])
        p_nat = sb("p_nat", [1, E])
        p_wide = sb("p_wide", [1, ER])
        ones = sb("ones", [1, N])
        p_col = sb("p_col", [P, 1])
        wide = yt[:, :, :, :].rearrange("p b n j -> p b (n j)").rearrange("p b (g q o) -> p b g q o", g=G, q=S)
        cw_wide, bias_wide = wide[:, 0, :, :, :], wide[0:1, 1, :, :, :]
        a_nat = y[:, :, :, :].rearrange("p c n j -> p (c n j)").rearrange("p (e q r) -> p e q r", e=E, q=S)
        b_nat = zb[:, 1, :]
        w_slots = [zb[:, 0, :], zb[:, 1, :], x_keep[:, 0, 0, :], x_keep[:, 0, 1, :],
                   x_keep[:, 1, 0, :], x_keep[:, 1, 1, :], b_rows[:, :]]
        w_sorted = [v.rearrange("p (k x) -> p k x", k=KT // 2)
                    for v in (w_spare[:, :], squares[:, :], yt[:, 0, :, :].rearrange("p n j -> p (n j)"),
                              yt[:, 1, :, :].rearrange("p n j -> p (n j)"))]

        z_ps = ctx.enter_context(nc.psum_tensor("z_ps", [P, H, BANK], F32))
        m_ps = ctx.enter_context(nc.psum_tensor("m_ps", [P, H, BANK], F32))
        conv_ps = [ctx.enter_context(nc.psum_tensor(f"conv_ps{i}", [P, BANK], F32)) for i in range(3)]
        side = ctx.enter_context(nc.psum_tensor("side", [P, BANK], F32))
        toep_ps, a_ps = conv_ps[0:2], [conv_ps[2], side]
        w_banks = [z_ps[:, 0, :], z_ps[:, 1, :], m_ps[:, 0, :], m_ps[:, 1, :]]

        small_loaded, b_rows_loaded = sem("small_loaded"), sem("b_rows_loaded")
        a_loaded, b_loaded = sem("a_loaded"), sem("b_loaded")
        w_loaded = [sem(f"w_loaded{i}") for i in range(OB)]
        ident_zero, ident_ready, w_pad_zero, w_pad_ready = (
            sem(s) for s in ("ident_zero", "ident_ready", "w_pad_zero", "w_pad_ready"))
        consts_set, x_diagonal = sem("consts_set"), sem("x_diagonal")
        cond_turned, cond_copied, widened, toep_placed, rows_summed, rows_copied = (
            sem(s) for s in ("cond_turned", "cond_copied", "widened", "toep_placed", "rows_summed", "rows_copied"))
        toep_hi_ready, toep_ready = sem("toep_hi_ready"), sem("toep_ready")
        pool_sorted, act_sorted = sem("pool_sorted"), sem("act_sorted")
        w_turned, w_hi_ready, w_ready, w_late_ready = (
            sem(s) for s in ("w_turned", "w_hi_ready", "w_ready", "w_late_ready"))
        a_permuted, a_hi_ready, a_ready, pb_scaled, pb_hi_ready, pb_ready = (
            sem(s) for s in ("a_permuted", "a_hi_ready", "a_ready", "pb_scaled", "pb_hi_ready", "pb_ready"))
        conv_done, u_done, z_done, m_done = sem("conv_done"), sem("u_done"), sem("z_done"), sem("m_done")
        x_edge_hi, x_hi_ready, y_hi_ready, u_hi_ready, squared = (
            sem(s) for s in ("x_edge_hi", "x_hi_ready", "y_hi_ready", "u_hi_ready", "squared"))
        x_ended, x_turned, x_back, x_edge_lo, x_cleared = (
            sem(s) for s in ("x_ended", "x_turned", "x_back", "x_edge_lo", "x_cleared"))
        x_kept, x_lo_ready, conv_biased, y_turned, y_lo_ready, u_lo_ready = (
            sem(s) for s in ("x_kept", "x_lo_ready", "conv_biased", "y_turned", "y_lo_ready", "u_lo_ready"))
        z_biased, gamma_steps, out_ready = sem("z_biased"), sem("gamma_steps"), sem("out_ready")
        z_free, m_free = sem("z_free"), sem("m_free")
        x_added, norms_ready, last_squared = sem("x_added"), sem("norms_ready"), sem("last_squared")
        exchanged = sem("exchanged")
        x_loaded = [sem(f"x_loaded{w}") for w in range(W2)]
        stored = [[sem(f"stored{s}{w}") for w in range(W2)] for s in range(2)]

        block = ctx.enter_context(nc.Block())

        def steps(engine, step):
            with engine.Fori(0, STEPS // 2 - 1) as pair:
                step(pair * 2 + 1, 1, pair + 1)
                step(pair * 2 + 2, 0, pair + 1)
            step(STEPS - 1, 1, STEPS // 2)

        def is_last(t):
            return isinstance(t, int) and t == STEPS - 1

        def lower(v):
            return v[0:P // 2]

        def x_half(g0):
            return xq[:, :].rearrange("p (a jb g0 jf) -> p a g0 jb jf", jb=JB, g0=2, jf=32)[:, :, g0, :, :]

        x_column0 = lower(xq[:, :].rearrange("p (a jb g0 jf) -> p a g0 jb jf", jb=JB, g0=2, jf=32)[:, :, :, 0, 0])

        def xs_parts(v, g0):
            return v[:, :, :, 0:J].rearrange("p n (gp g0) (jb jf) -> p (n gp) g0 jb jf", g0=2, jf=32)[:, :, g0, :, :]

        def xs_last(v):
            return lower(v[:, :, :, J].rearrange("p n (gp g0) -> p (n gp) g0", g0=2))

        def toep_part(c, q0):
            hi, lo = (v[:, :, c, :].rearrange("p g (qq q0 o) -> p g qq q0 o", qq=4, q0=Q0)[:, :, :, q0, :]
                      for v in (toep_hi, toep_lo))
            nat = toep_ps[c][:, :].rearrange("p (q0 qq g o) -> p q0 g qq o", q0=Q0, qq=4, g=G)
            return hi, lo, nat[:, q0, :, :, :]

        POOL_SORTS, ACT_SORTS = (1, 3, 5, 7, 9, 11, 13), (0, 2, 4, 6, 8, 10, 12, 14, 15)

        def sorted_by(k):
            for sorts, signal in ((POOL_SORTS, pool_sorted), (ACT_SORTS, act_sorted)):
                if k in sorts:
                    return signal, sorts.index(k) + 1

        W_LATE = 2 * OB - 6

        def w_bank(k):
            return w_banks[k % 4] if k < W_LATE else (
                w_banks[2], w_banks[3], conv_ps[1], conv_ps[2], conv_ps[0], w_banks[1])[k - W_LATE]

        def w_bank_free(k):
            if k < W_LATE:
                return w_ready, k - 3
            return ((w_ready, W_LATE - 3), (w_ready, W_LATE - 2), (conv_biased, 2), (conv_biased, 3),
                    (conv_biased, 4), (w_ready, W_LATE))[k - W_LATE]

        def w_whole(k):
            v = [x_keep[:, 1, 0, 0:BANK], x_keep[:, 1, 0, BANK:], x_keep[:, 1, 1, 0:BANK],
                 x_keep[:, 1, 1, BANK:], w_spare[:, :], squares[:, :]][k - W_LATE]
            return v.rearrange("p (q o) -> p q o", q=4)

        def w_in_order(k):
            if k in (W_LATE, W_LATE + 1):
                a = k - W_LATE
                return zb[:, 1, a * BANK:(a + 1) * BANK].rearrange("p (q o) -> p q o", q=4)
            return w_sorted[k % 4] if k < 2 * OB - 2 else w_whole(k - 2)

        def w_part(v, k):
            ob, h = divmod(k, 2)
            return v[:, 4 * h:4 * h + 4, ob * P:(ob + 1) * P]

        def sort_w(engine, copy, k):
            ob, h = divmod(k, 2)
            engine.wait_ge(w_loaded[ob], 16)
            if k in (2, 3):
                engine.wait_ge(rows_summed, 1)
            if k >= 4:
                engine.wait_ge(w_turned, k - 3 if k < 2 * OB - 2 else 2 * OB - 4)
            for a in range(2):
                jb = 2 * h + a
                part = w_slots[ob % len(w_slots)][:, jb * 32 * S:(jb + 1) * 32 * S].rearrange("p (jf q) -> p q jf", q=S)
                dst = w_in_order(k)[:, a * Q0:(a + 1) * Q0, :].rearrange(
                    "p k (qq jf) -> p (k qq) jf", qq=4)
                last = copy(dst, part)
            last.then_inc(sorted_by(k)[0], 1)

        def add_x(engine, f, par, w):
            engine.wait_ge(z_biased, 4 * f + 2 * w + 2)
            engine.tensor_tensor(x_keep[:, par, w, :], x_keep[:, par, w, :], zb[:, w, :],
                                 ALU.add).then_inc(x_added, 1)

        def exchange_part(a, b):
            return (xq[32 * a:32 * a + 32, :].rearrange("p (w b x) -> p w b x", w=W2, b=4)[:, :, b, :],
                    xe[32 * b:32 * b + 32, :].rearrange("p (w a x) -> p w a x", w=W2, a=4)[:, :, a, :])

        def keep_diagonal(engine, copy, t):
            engine.wait_ge(x_turned, 4 * t + 4)
            if not (isinstance(t, int) and t == 0):
                engine.wait_ge(x_back, t)
            for a in range(4):
                src, dst = exchange_part(a, a)
                copy(dst, src).then_inc(x_diagonal, 1)

        LAST = W2 * STEPS - 1

        def half_of(v, h):
            return v[:, h * BANK:(h + 1) * BANK]

        @block.sync
        def _(sp):
            def load_x(tile, w):
                sp.dma_start(x_in[:, w, PAD:XP],
                             x_tiles[bass.ds(tile, 1), :, :].rearrange("a p l -> (a p) l")
                             ).then_inc(x_loaded[w], 16)

            def snapped(value):
                return value if isinstance(value, int) else sp.snap(value)

            def load_w(ob):
                sp.dma_start(w_slots[ob % len(w_slots)], ffn_w[ob * P:(ob + 1) * P, :]).then_inc(w_loaded[ob], 16)

            for w in range(W2):
                sp.sem_inc(stored[1][w], 16)
            for w in range(W2):
                load_x(w, w)
            sp.dma_start(conv_nat, conv_w.rearrange("o i k -> o (i k)")).then_inc(small_loaded, 16)
            sp.dma_start(cond_nat, cond).then_inc(small_loaded, 16)
            sp.dma_start(cond_w_nat, cond_w).then_inc(small_loaded, 16)
            sp.dma_start(bias_nat[:, :], bias.rearrange("(a o) -> a o", a=1)).then_inc(small_loaded, 16)
            sp.dma_start(p_nat[:, :], p_scores.rearrange("(a e) -> a e", a=1)).then_inc(small_loaded, 16)
            for ob in range(OB // 2 + 1):
                load_w(ob)
                if ob == OB // 2 - 1:
                    sp.dma_start(a_nat, ffn_a.rearrange("e (j q) r -> j e q r", q=S)).then_inc(a_loaded, 16)

            def load_next(t, w):
                tile, turned, kept = (snapped(v) for v in (W2 * t + W2 + w, 4 * t + 2 * w + 2, W2 * t + w + 1))
                sp.wait_ge(x_turned, turned)
                sp.wait_ge(x_kept, kept)
                load_x(tile, w)

            def exchange(t):
                first = isinstance(t, int) and t == 0
                turned, free = (snapped(v) for v in (4 * t + 4, t))
                sp.wait_ge(x_turned, turned)
                if not first:
                    sp.wait_ge(x_back, free)
                for a in range(4):
                    for b in range(4):
                        if a != b:
                            src, dst = exchange_part(a, b)
                            sp.dma_start(dst, src).then_inc(exchanged, 16)

            exchange(0)
            sp.wait_ge(cond_turned, 1)
            sp.wait_ge(w_pad_ready, 1)
            for ob in range(OB // 2 + 1, OB - 1):
                load_w(ob)
            sp.wait_ge(w_turned, 2)
            load_w(OB - 1)
            for w in range(W2):
                load_next(0, w)

            def store(f, par, w):
                tile, whole = (snapped(v) for v in (W2 * f + w, W2 * f + w + 1))
                sp.wait_ge(out_ready, whole)
                sp.dma_start(out_tiles[bass.ds(tile, 1), :, :].rearrange("a p l -> (a p) l"),
                             x_keep[:, par, w, :]).then_inc(stored[par][w], 16)

            exchange(1)
            sp.wait_ge(w_turned, 14)
            sp.dma_start(b_rows[:, :], ffn_b.rearrange("(a o) -> a o", a=1).partition_broadcast(P)
                         ).then_inc(b_rows_loaded, 16)
            sp.dma_start(b_nat, ffn_bm.rearrange("e r o -> (e r) o")).then_inc(b_loaded, 16)
            with sp.Fori(0, STEPS // 2 - 1) as pair:
                for par in (1, 0):
                    t = pair * 2 + (2 - par)
                    for w in range(W2):
                        load_next(t, w)
                    exchange(t + 1)
                    for w in range(W2):
                        store(t - 1, 1 - par, w)
            for w in range(W2):
                store(STEPS - 2, 0, w)
            store(STEPS - 1, 1, 0)
            for h in range(H):
                sp.wait_ge(out_ready, LAST + 1 + h)
                sp.dma_start(half_of(out_tiles[LAST, :, :], h),
                             half_of(x_keep[:, 1, 1, :], h)).then_inc(stored[1][1], 16)
            for w in range(W2):
                sp.wait_ge(stored[0][w], 16 * (STEPS // 2))
                sp.wait_ge(stored[1][w], 16 * (STEPS // 2) + 16 + 16 * w)

        @block.tensor
        def _(pe):
            def three(ps, pairs, first=True, last=True):
                for i, (lh, ll, rh, rl) in enumerate(pairs):
                    for k, (a, b) in enumerate(((lh, rh), (lh, rl), (ll, rh))):
                        mm = pe.matmul(ps, a, b, start=(first and i == 0 and k == 0),
                                       stop=(last and i == len(pairs) - 1 and k == 2))
                return mm

            def conv(t, g):
                first = isinstance(t, int) and t == 0
                if g == 0:
                    pe.wait_ge(x_lo_ready, W2 * t + W2)
                if g == 3:
                    pe.wait_ge(conv_biased, 4 * t + 1)
                elif not first:
                    pe.wait_ge(conv_biased, 4 * t - 4 + (4, 2, 3)[g])
                three(conv_ps[g % 3][:, :].rearrange("p (n j) -> p n j", n=NB),
                      [(toep_hi[:, g, c, :], toep_lo[:, g, c, :],
                        xs_hi[:, :, g, c:c + J], xs_lo[:, :, g, c:c + J]) for c in range(2)]
                      ).then_inc(conv_done, 1)

            def u(f, par):
                pe.wait_ge(y_lo_ready, 4 * f + 4)
                three(side[:, 0:W2 * P],
                      [(a_hi[:, q, :], a_lo[:, q, :], yT_hi[:, par, q, :], yT_lo[:, par, q, :])
                       for q in range(KT)]).then_inc(u_done, 1)

            def z(f, par, w, h, part):
                if part == 0:
                    if h == H - 1:
                        pe.wait_ge(w_late_ready, 2 * OB - W_LATE)
                    pe.wait_ge(z_free, 4 * f + 2 * w + h + 1)
                rows, cols = slice(w * P, (w + 1) * P), slice(h * BANK, (h + 1) * BANK)
                mm = three(z_ps[:, h, :],
                           [(yT_hi[:, par, q, rows], yT_lo[:, par, q, rows],
                             wt_hi[:, q, cols], wt_lo[:, q, cols]) for q in (2 * part, 2 * part + 1)],
                           first=(part == 0), last=(part == 3))
                if part == 3:
                    mm.then_inc(z_done, 1)

            def m(f, w):
                if w == 0:
                    pe.wait_ge(pb_ready, 1)
                    pe.wait_ge(u_lo_ready, f + 1)
                pe.wait_ge(m_free, W2 * f + w + 1)
                rows = slice(w * P, (w + 1) * P)
                for h in range(H):
                    cols = slice(h * BANK, (h + 1) * BANK)
                    mm = three(m_ps[:, h, :],
                               [(u_hi[:, rows], u_lo[:, rows], pb_hi[:, cols], pb_lo[:, cols])])
                mm.then_inc(m_done, 1)

            FILL_SMALL, FILL_WIDENED, FILL_X, FILL_LATE = 26, 16, 24, 6

            def keep_warm(bank, count):
                for _ in range(count):
                    pe.transpose(bank[:, 0:P], ident[:, :], ident[:, :])

            pe.wait_ge(ident_ready, 1)
            keep_warm(w_banks[0], FILL_SMALL)
            pe.wait_ge(small_loaded, 16 * 5)
            pe.transpose(side[:, 0:N], cond_nat, ident[0:N, 0:N])
            pe.transpose(side[:, N:N + CO], cond_w_nat, ident[0:CO, 0:CO]).then_inc(cond_turned, 1)
            keep_warm(w_banks[0], FILL_WIDENED)
            pe.wait_ge(cond_copied, 1)
            pe.wait_ge(widened, 3)
            pe.wait_ge(consts_set, 1)
            for g in range(G):
                pe.matmul(side[:, N * g:N * (g + 1)], cw_wide[:, g, :, :].rearrange("d q o -> d (q o)"),
                          condT[:, 0:N], start=True, stop=False)
                pe.matmul(side[:, N * g:N * (g + 1)],
                          bias_wide[:, g, :, :].rearrange("d q o -> d (q o)"), ones[:, :],
                          start=False, stop=True)
            pe.matmul(a_ps[0][:, 0:2], p_wide[:, :], ones[:, 0:2], start=True, stop=True).then_inc(rows_summed, 1)

            def place_toep(c):
                pe.wait_ge(w_pad_ready, 1)
                for q in range(S):
                    first = S * c + S - 1 - q
                    mm = pe.matmul(toep_ps[c][:, q * CO:(q + 1) * CO],
                                   w_pad[:, first:first + S, :].rearrange("o k i -> o (k i)"),
                                   ident[0:CO, 0:CO], start=True, stop=True)
                mm.then_inc(toep_placed, 1)

            def permute_a(part):
                for jb in (2 * part, 2 * part + 1):
                    for q0 in range(Q0):
                        kt = jb * Q0 + q0
                        cols = slice(kt % 4 * ER, (kt % 4 + 1) * ER)
                        for qq in range(4):
                            mm = pe.matmul(a_ps[part][32 * qq:32 * qq + 32, cols], ident[:, 32 * jb:32 * jb + 32],
                                           a_nat[:, :, 4 * q0 + qq, :], start=True, stop=True)
                mm.then_inc(a_permuted, 1)

            def turn_w(k):
                pe.wait_ge(*sorted_by(k))
                if k >= 4:
                    pe.wait_ge(*w_bank_free(k))
                for a in range(4):
                    tr = pe.transpose(w_bank(k)[:, a * P:(a + 1) * P], w_in_order(k)[:, a, :], ident[:, :])
                tr.then_inc(w_turned, 1)

            for k in range(8):
                turn_w(k)
                if k in (1, 3):
                    place_toep(k // 2)
            pe.wait_ge(a_loaded, 16)
            pe.wait_ge(rows_copied, 1)
            for part in range(2):
                permute_a(part)
            pe.wait_ge(toep_ready, 2)
            keep_warm(conv_ps[0], FILL_X)
            conv(0, 0)
            turn_w(8)
            conv(0, 1)
            turn_w(9)
            pe.wait_ge(a_ready, 2)
            conv(0, 2)
            conv(0, 3)
            for k in range(W_LATE, 2 * OB):
                turn_w(k)
                if k % 2:
                    keep_warm(side, FILL_LATE)
            pe.wait_ge(w_ready, W_LATE)

            def step(t, par, turn):
                f, fp = t - 1, 1 - par
                u(f, fp)
                for part in range(4):
                    z(f, fp, 0, 0, part)
                for part in range(3):
                    z(f, fp, 0, 1, part)
                conv(t, 0)
                z(f, fp, 0, 1, 3)
                m(f, 0)
                conv(t, 1)
                z(f, fp, 1, 0, 0)
                conv(t, 2)
                z(f, fp, 1, 0, 1)
                conv(t, 3)
                for part in range(2, 4):
                    z(f, fp, 1, 0, part)
                for part in range(4):
                    z(f, fp, 1, 1, part)
                m(f, 1)

            steps(pe, step)
            u(STEPS - 1, 1)
            for w in range(W2):
                for h in range(H):
                    if (w, h) == (W2 - 1, H - 1):
                        m(STEPS - 1, w)
                    for part in range(4):
                        z(STEPS - 1, 1, w, h, part)
                if w < W2 - 1:
                    m(STEPS - 1, w)

        @block.scalar
        def _(act):
            def copy(dst, src):
                return act.activation(dst, src, ACT.Copy)

            def x_edge_high(t):
                act.wait_ge(x_back, t + 1)
                if not (isinstance(t, int) and t == 0):
                    act.wait_ge(conv_done, 4 * t)
                copy(xs_last(xs_hi), x_column0).then_inc(x_edge_hi, 1)

            def x_high(t, g0):
                act.wait_ge(x_cleared, t + 1)
                copy(xs_parts(xs_hi, g0), x_half(g0)).then_inc(x_hi_ready, 1)

            def y_high(t, par, g):
                act.wait_ge(y_turned, 4 * t + g + 1)
                yv = yT_hi[:, par, :, :].rearrange("p k (n g o) -> p g n k o", n=NB, g=G)
                copy(yv[:, g, :, :, :],
                     yt[:, g % 2, :, :].rearrange("p n (k o) -> p n k o", k=KT)).then_inc(y_hi_ready, 1)

            def u_high(f):
                act.wait_ge(u_done, f + 1)
                copy(u_hi[:, :], side[:, 0:W2 * P]).then_inc(u_hi_ready, 1)

            def square_z(f, w):
                act.wait_ge(z_biased, 4 * f + 2 * w + 2)
                act.activation(squares[:, :].bitcast(BF16), zb[:, w, :], ACT.Square,
                               accum_out=ssq[:, w, 0:1]).then_inc(squared, 1)

            def square_m(f, w, after_z=True):
                act.wait_ge(squared, 4 * f + 2 * w + after_z)
                act.wait_ge(m_done, W2 * f + w + 1)
                act.activation(squares[:, :].bitcast(BF16), m_ps[:, :, :].rearrange("p h c -> p (h c)"), ACT.Square,
                               accum_out=ssq[:, w, 1:2]).then_inc(squared, 1)

            def w_high(k):
                act.wait_ge(w_turned, k + 1)
                if k >= W_LATE:
                    act.wait_ge(w_turned, 2 * OB)
                    copy(w_whole(k), w_bank(k).rearrange("p (q o) -> p q o", q=4))
                copy(w_part(wt_hi, k), w_bank(k).rearrange("p (q o) -> p q o", q=4)).then_inc(w_hi_ready, 1)

            def sort(k):
                sort_w(act, copy, k)

            def a_high(part):
                act.wait_ge(a_permuted, part + 1)
                copy(a_hi[:, 4 * part:4 * part + 4, :],
                     a_ps[part][:, :].rearrange("p (k x) -> p k x", x=ER)).then_inc(a_hi_ready, 1)

            def bias_conv(g):
                act.wait_ge(conv_done, g + 1)
                if g >= 2:
                    act.wait_ge(y_turned, g - 1)
                for n in range(NB):
                    last = act.activation(y[:, g % 2, n, :], conv_ps[g % 3][:, n * J:(n + 1) * J], ACT.Identity,
                                          bias=row_add[:, g, n:n + 1])
                last.then_inc(conv_biased, 1)

            def toep_high(c):
                act.wait_ge(toep_placed, c + 1)
                for q0 in range(Q0):
                    hi, _, nat = toep_part(c, q0)
                    last = copy(hi, nat)
                last.then_inc(toep_hi_ready, 1)

            act.wait_ge(cond_turned, 1)
            copy(condT[:, :], side[0:D, 0:N + CO]).then_inc(cond_copied, 1)
            act.wait_ge(cond_copied, 1)
            copy(cw_wide[:, :, :, :],
                 condT[:, N:N + CO].rearrange("d (g o) -> d g o", g=G).unsqueeze(2)
                 .to_broadcast([D, G, S, OG])).then_inc(widened, 1)
            act.wait_ge(small_loaded, 16 * 5)
            copy(bias_wide[:, :, :, :],
                 bias_nat[:, :].rearrange("a (g o) -> a g o", g=G).unsqueeze(2)
                 .to_broadcast([1, G, S, OG])).then_inc(widened, 1)
            copy(p_wide[:, :].rearrange("a (e r) -> a e r", e=E),
                 p_nat[:, :].unsqueeze(2).to_broadcast([1, E, R])).then_inc(widened, 1)
            act.wait_ge(w_pad_zero, 1)
            copy(w_pad[:, S - 1:S - 1 + K, :],
                 conv_nat.rearrange("o (i k) -> o k i", k=K)).then_inc(w_pad_ready, 1)
            sort(0)
            act.wait_ge(rows_summed, 1)
            copy(row_add[:, :, :], side[:, 0:G * N].rearrange("p (g n) -> p g n", g=G))
            copy(p_col[:, :], a_ps[0][:, 0:1]).then_inc(rows_copied, 1)
            for ob in range(4):
                sort(2 * ob + 2)
                w_high(2 * ob)
                w_high(2 * ob + 1)
                if ob < 2:
                    toep_high(ob)
            x_edge_high(0)
            x_high(0, 0)
            x_high(0, 1)
            for part in range(2):
                a_high(part)
            sort(10)
            bias_conv(0)
            w_high(8)
            sort(12)
            bias_conv(1)
            y_high(0, 0, 0)
            w_high(9)
            bias_conv(2)
            y_high(0, 0, 1)
            sort(14)
            bias_conv(3)
            y_high(0, 0, 2)
            sort(15)
            y_high(0, 0, 3)
            for k in range(W_LATE, 2 * OB):
                w_high(k)
            x_edge_high(1)
            for g0 in range(2):
                x_high(1, g0)
            act.wait_ge(b_loaded, 16)
            act.activation(b_nat, b_nat, ACT.Copy, scale=p_col[:, :]).then_inc(pb_scaled, 1)
            act.wait_ge(pb_scaled, 1)
            copy(pb_hi[:, :], b_nat).then_inc(pb_hi_ready, 1)
            act.wait_ge(w_late_ready, 2 * OB - W_LATE)

            def step(t, par, turn):
                f = t - 1
                u_high(f)
                square_z(f, 0)
                y_high(t, par, 0)
                square_m(f, 0)
                y_high(t, par, 1)
                if not is_last(t):
                    keep_diagonal(act, copy, t + 1)
                for g in range(2, G):
                    y_high(t, par, g)
                square_z(f, 1)
                square_m(f, 1)
                if not is_last(t):
                    x_edge_high(t + 1)
                    for g0 in range(2):
                        x_high(t + 1, g0)

            steps(act, step)
            u_high(STEPS - 1)
            square_z(STEPS - 1, 0)
            square_m(STEPS - 1, 0)
            square_m(STEPS - 1, 1, after_z=False)
            for h in range(H):
                act.wait_ge(squared, 2 * LAST + 1 + h)
                act.wait_ge(z_biased, 2 * LAST + 1 + h)
                act.activation(half_of(squares[:, :].bitcast(BF16), h), half_of(zb[:, 1, :], h), ACT.Square,
                               accum_out=(ssq[:, 1, 0:1], ssq_half[:, :])[h]).then_inc(squared, 1)

        @block.vector
        def _(dve):
            def rest(dst, whole, high):
                return dve.tensor_tensor(dst, whole, high.bitcast(F32), ALU.subtract)

            def keep_x(t, par, w, stores):
                dve.wait_ge(x_loaded[w], 16 * t + 16)
                if stores is not None:
                    dve.wait_ge(stored[par][w], 16 * stores)
                dve.tensor_copy(x_keep[:, par, w, :], x_in[:, w, PAD:XP]).then_inc(x_kept, 1)

            def turn_x(t):
                first = isinstance(t, int) and t == 0
                for w in range(W2):
                    dve.wait_ge(x_loaded[w], 16 * t + 16)
                dve.tensor_copy(x_in[:, :, 0:PAD], x_in[:, :, L:XP]).then_inc(x_ended, 1)
                dve.wait_ge(x_ended, t + 1)
                if not first:
                    dve.wait_ge(x_lo_ready, 2 * t)
                for w in range(W2):
                    rows = x_in[:, w, 0:L].rearrange("p (jb jf sp s0) -> p s0 sp jb jf", jf=32, sp=4, s0=2)
                    turned = xq[:, w * L:(w + 1) * L].rearrange("p (b g0 s0 i) -> p s0 b g0 i", g0=2, s0=2, i=CI)
                    for s0 in range(2):
                        dve.transpose(turned[:, s0, :, :, :], rows[:, s0, :, :, :]).then_inc(x_turned, 1)

            def turn_back(t):
                dve.wait_ge(x_diagonal, 4 * t + 4)
                dve.wait_ge(exchanged, 192 * t + 192)
                dve.transpose(xq[:, :], xe[:, :]).then_inc(x_back, 1)

            def x_edge_low(t):
                dve.wait_ge(x_edge_hi, t + 1)
                rest(xs_last(xs_lo), x_column0, xs_last(xs_hi)).then_inc(x_edge_lo, 1)
                dve.wait_ge(x_edge_lo, t + 1)
                dve.memset(x_column0, 0.0).then_inc(x_cleared, 1)

            def x_low(t, g0):
                dve.wait_ge(x_hi_ready, 2 * t + g0 + 1)
                rest(xs_parts(xs_lo, g0), x_half(g0), xs_parts(xs_hi, g0)).then_inc(x_lo_ready, 1)

            def conv_bias(t, g):
                dve.wait_ge(conv_done, 4 * t + g + 1)
                dve.wait_ge(y_turned, 4 * t + g - 1)
                dve.tensor_tensor(y[:, g % 2, :, :],
                                  conv_ps[g % 3][:, :].rearrange("p (n j) -> p n j", n=NB),
                                  row_add[:, g, bass.ds(t * NB, NB)].unsqueeze(2).to_broadcast([P, NB, J]),
                                  ALU.add).then_inc(conv_biased, 1)

            def turn_y(t, g):
                first = isinstance(t, int) and t == 0
                dve.wait_ge(conv_biased, 4 * t + g + 1)
                if not first or g >= 2:
                    dve.wait_ge(y_lo_ready, 4 * t + g - 1)
                dve.transpose(yt[:, g % 2, :, :].rearrange("p n j -> p (n j)"),
                              y[:, g % 2, :, :].rearrange("p n j -> p (n j)")).then_inc(y_turned, 1)

            def y_low(t, par, g):
                dve.wait_ge(y_hi_ready, 4 * t + g + 1)
                lo, hi = (v[:, par, :, :].rearrange("p k (n g o) -> p g n k o", n=NB, g=G)[:, g, :, :, :]
                          for v in (yT_lo, yT_hi))
                rest(lo, yt[:, g % 2, :, :].rearrange("p n (k o) -> p n k o", k=KT), hi).then_inc(y_lo_ready, 1)

            def biased_turned(t, g):
                conv_bias(t, g)
                turn_y(t, g)

            def u_low(f):
                dve.wait_ge(u_hi_ready, f + 1)
                rest(u_lo[:, :], side[:, 0:W2 * P], u_hi[:, :]).then_inc(u_lo_ready, 1)

            def z_bias(f, w, h):
                dve.wait_ge(z_done, 4 * f + 2 * w + h + 1)
                cols = slice(h * BANK, (h + 1) * BANK)
                dve.tensor_tensor(zb[:, w, cols], z_ps[:, h, :], b_rows[:, cols],
                                  ALU.add).then_inc(z_biased, 1)
                dve.wait_ge(z_biased, 4 * f + 2 * w + h + 1)
                dve.sem_inc(z_free, 1)

            def work_gamma(f, w):
                tile = W2 * f + w
                dve.wait_ge(norms_ready, tile + 1)
                dve.tensor_scalar(den[:, w:w + 1], norms[:, w, 1:2], EPS, 1 / C_CLAMP,
                                  ALU.add, ALU.mult).then_inc(gamma_steps, 1)
                dve.wait_ge(gamma_steps, 3 * tile + 1)
                dve.reciprocal(rden[:, w:w + 1], den[:, w:w + 1]).then_inc(gamma_steps, 1)
                dve.wait_ge(gamma_steps, 3 * tile + 2)
                dve.tensor_scalar(gamma[:, w:w + 1], norms[:, w, 0:1], rden[:, w:w + 1], 1.0,
                                  ALU.mult, ALU.min).then_inc(gamma_steps, 1)
                dve.wait_ge(gamma_steps, 3 * tile + 3)

            def finish(f, par, w):
                tile = W2 * f + w
                work_gamma(f, w)
                dve.wait_ge(x_added, tile + 1)
                dve.scalar_tensor_tensor(x_keep[:, par, w, :], m_ps[:, :, :].rearrange("p h c -> p (h c)"),
                                         gamma[:, w:w + 1], x_keep[:, par, w, :],
                                         ALU.mult, ALU.add).then_inc(out_ready, 1)
                dve.wait_ge(out_ready, tile + 1)
                dve.sem_inc(m_free, 1)

            dve.sem_inc(z_free, 2)
            dve.sem_inc(m_free, 1)
            dve.memset(xs_hi[P // 2:P, :, :, J].bitcast(F32), 0.0)
            dve.memset(xs_lo[P // 2:P, :, :, J].bitcast(F32), 0.0)
            dve.memset(half[:, :], 0.5)
            dve.memset(ones[:, :], 1.0).then_inc(consts_set, 1)
            turn_x(0)
            def w_low(k):
                dve.wait_ge(w_hi_ready, k + 1)
                rest(w_part(wt_lo, k), w_bank(k).rearrange("p (q o) -> p q o", q=4),
                     w_part(wt_hi, k)).then_inc(w_ready, 1)

            def a_low(part):
                dve.wait_ge(a_hi_ready, part + 1)
                cols = (slice(None), slice(4 * part, 4 * part + 4))
                rest(a_lo[cols], a_ps[part][:, :].rearrange("p (k x) -> p k x", x=ER), a_hi[cols]
                     ).then_inc(a_ready, 1)

            def toep_low(c):
                dve.wait_ge(toep_hi_ready, c + 1)
                for q0 in range(Q0):
                    hi, lo, nat = toep_part(c, q0)
                    last = rest(lo, nat, hi)
                last.then_inc(toep_ready, 1)

            keep_diagonal(dve, dve.tensor_copy, 0)
            for k in range(4):
                w_low(k)
                if k in (1, 3):
                    toep_low(k // 2)
            turn_back(0)
            x_edge_low(0)
            dve.wait_ge(w_turned, 8)
            for w in range(W2):
                keep_x(0, 0, w, None)
            for g0 in range(2):
                x_low(0, g0)
            w_low(4)
            w_low(5)
            for part in range(2):
                a_low(part)
            turn_y(0, 0)
            turn_x(1)
            w_low(6)
            w_low(7)
            turn_y(0, 1)
            y_low(0, 0, 0)
            w_low(8)
            turn_y(0, 2)
            y_low(0, 0, 1)
            w_low(9)
            turn_y(0, 3)
            y_low(0, 0, 2)
            y_low(0, 0, 3)
            keep_diagonal(dve, dve.tensor_copy, 1)
            turn_back(1)
            x_edge_low(1)
            for g0 in range(2):
                x_low(1, g0)
            dve.wait_ge(pb_hi_ready, 1)
            rest(pb_lo[:, :], b_nat, pb_hi[:, :]).then_inc(pb_ready, 1)
            dve.wait_ge(b_rows_loaded, 16)
            dve.wait_ge(w_late_ready, 2 * OB - W_LATE)

            def step(t, par, turn):
                f = t - 1
                u_low(f)
                for w in range(W2):
                    keep_x(t, par, w, turn)
                z_bias(f, 0, 0)
                biased_turned(t, 0)
                z_bias(f, 0, 1)
                if not is_last(t):
                    turn_x(t + 1)
                biased_turned(t, 1)
                y_low(t, par, 0)
                biased_turned(t, 2)
                y_low(t, par, 1)
                finish(f, 1 - par, 0)
                biased_turned(t, 3)
                y_low(t, par, 2)
                y_low(t, par, 3)
                z_bias(f, 1, 0)
                z_bias(f, 1, 1)
                if not is_last(t):
                    turn_back(t + 1)
                    x_edge_low(t + 1)
                finish(f, 1 - par, 1)
                if not is_last(t):
                    for g0 in range(2):
                        x_low(t + 1, g0)

            steps(dve, step)
            u_low(STEPS - 1)
            for w in range(W2):
                for h in range(H):
                    z_bias(STEPS - 1, w, h)
                    if w == W2 - 1:
                        dve.tensor_tensor(half_of(x_keep[:, 1, w, :], h), half_of(x_keep[:, 1, w, :], h),
                                          half_of(zb[:, w, :], h), ALU.add).then_inc(x_added, 1)
                if w < W2 - 1:
                    finish(STEPS - 1, 1, w)
            dve.wait_ge(squared, 2 * LAST + 3)
            dve.tensor_tensor(ssq[:, 1, 0:1], ssq[:, 1, 0:1], ssq_half[:, :], ALU.add).then_inc(last_squared, 1)
            work_gamma(STEPS - 1, 1)
            dve.wait_ge(x_added, LAST + 2)
            for h in range(H):
                dve.scalar_tensor_tensor(half_of(x_keep[:, 1, 1, :], h), m_ps[:, h, :], gamma[:, 1:2],
                                         half_of(x_keep[:, 1, 1, :], h), ALU.mult, ALU.add).then_inc(out_ready, 1)

        @block.gpsimd
        def _(pool):
            def roots(f, w):
                if isinstance(f, int) and W2 * f + w == LAST:
                    pool.wait_ge(last_squared, 1)
                else:
                    pool.wait_ge(squared, 4 * f + 2 * w + 2)
                pool.tensor_tensor(norms[:, w, :], ssq[:, w, :], half[:, :], ALU.pow).then_inc(norms_ready, 1)

            pool.memset(w_pad[:, :, :], 0.0).then_inc(w_pad_zero, 1)
            pool.memset(ident[:, :], 0.0).then_inc(ident_zero, 1)
            pool.wait_ge(ident_zero, 1)
            pool.affine_select(out=ident[:, :], in_=ident[:, :], compare_op=ALU.not_equal, fill=1.0, base=0,
                               pattern=[[-1, P]], channel_multiplier=1).then_inc(ident_ready, 1)
            for k in POOL_SORTS:
                sort_w(pool, pool.tensor_copy, k)
            for k in range(W_LATE, 2 * OB):
                pool.wait_ge(w_hi_ready, k + 1)
                pool.tensor_tensor(w_part(wt_lo, k), w_whole(k),
                                   w_part(wt_hi, k).bitcast(F32), ALU.subtract).then_inc(w_late_ready, 1)
            pool.wait_ge(consts_set, 1)
            with pool.Fori(0, STEPS // 2 - 1) as pair:
                for par in (1, 0):
                    t = pair * 2 + (2 - par)
                    for w in range(W2):
                        add_x(pool, t - 1, 1 - par, w)
                        roots(t - 1, w)
            for f, par in ((STEPS - 2, 0), (STEPS - 1, 1)):
                for w in range(W2):
                    if (f, w) != (STEPS - 1, W2 - 1):
                        add_x(pool, f, par, w)
                    roots(f, w)


_INS = ["x", "cond_128", "fside_S_0", "L0_cond_weight", "L0_cond_c_weight", "L0_ffn_W", "L0_ffn_b",
        "L0_ffn_A", "L0_ffn_B", "L0_ffn_p_scores"]


def kernel(**inputs):
    import numpy as np
    import concourse.bacc as bacc
    from concourse.bass_utils import run_bass_kernel_spmd

    nc = bacc.Bacc("TRN2", target_bir_lowering=False, num_devices=1)
    arrays, args = {}, []
    for name in _INS:
        a = np.ascontiguousarray(inputs[name])
        arrays[f"in_{name}"] = a
        args.append(nc.dram_tensor(f"in_{name}", a.shape, mybir.dt.from_np(a.dtype), kind="ExternalInput").ap())
    shape = inputs["x"].shape
    out = nc.dram_tensor("out", shape, F32, kind="ExternalOutput").ap()
    build(nc, *args, out)
    r = run_bass_kernel_spmd(nc, [arrays], core_ids=[0])
    return r.results[0]["out"]
```
